# Optimizing a Trainium2 kernel written in Bass

```python
import numpy as np
import jax
import jax.numpy as jnp

def _softmax(x, axis=-1):
    return jax.nn.softmax(x, axis=axis)

def _gelu(x):
    return jax.nn.gelu(x, approximate=True)

def _silu(x):
    return jax.nn.silu(x)

def _sigmoid(x):
    return jax.nn.sigmoid(x)

def _layernorm(x, axis=-1, eps=1e-05):
    m = jnp.mean(x, axis=axis, keepdims=True)
    v = jnp.var(x, axis=axis, keepdims=True)
    return (x - m) / jnp.sqrt(v + eps)

def _scatter_add(tgt, idx, src, axis=0):
    return tgt.at[idx].add(src)

def _segment_sum(src, seg, n):
    return jax.ops.segment_sum(src, seg, n)
kernel_name = 'mk_prb_d1_jaxref_r8_92d24f'

def setup_inputs(seed: int=0):
    np.random.seed(seed)
    _w = jnp.asarray

    def _L0_attn_setup():
        import math
        import jax, jax.numpy as jnp
        import numpy as np
        L, D, H, F = (4, 128, 16, 512)
        HD = D // H
        EPS = 1e-05

        def get_alibi_slopes(num_heads):
            closest = 2 ** math.floor(math.log2(num_heads))
            base = 2 ** (-2 ** (-(math.log2(closest) - 3)))
            slopes = base ** np.arange(1, closest + 1)
            if closest != num_heads:
                extra_base = 2 ** (-2 ** (-(math.log2(2 * closest) - 3)))
                extra = extra_base ** np.arange(1, 2 * (num_heads - closest) + 1, 2)
                slopes = np.concatenate([slopes, extra])
            return jnp.asarray(slopes, dtype=jnp.float32)

        def build_mask(num_heads, T):
            pos = jnp.arange(T)
            dist = pos[None, :] - pos[:, None]
            alibi = get_alibi_slopes(num_heads)[:, None, None] * dist[None]
            causal = jnp.where(dist > 0, -jnp.inf, 0.0).astype(jnp.float32)
            return causal[None] + alibi

        def layer_norm(x, w, b):
            mu = jnp.mean(x, axis=-1, keepdims=True)
            var = jnp.mean(jnp.square(x - mu), axis=-1, keepdims=True)
            return (x - mu) * jax.lax.rsqrt(var + EPS) * w + b

        def mha(x, mask, Wi, bi, Wo, bo):
            B, T, _ = x.shape
            qkv = x @ Wi.T + bi
            q, k, v = jnp.split(qkv, 3, axis=-1)
            q = q.reshape(B, T, H, HD).transpose(0, 2, 1, 3)
            k = k.reshape(B, T, H, HD).transpose(0, 2, 1, 3)
            v = v.reshape(B, T, H, HD).transpose(0, 2, 1, 3)
            scores = jnp.einsum('bhqd,bhkd->bhqk', q, k) / math.sqrt(HD)
            scores = scores + mask[None]
            attn = jax.nn.softmax(scores, axis=-1)
            out = jnp.einsum('bhqk,bhkd->bhqd', attn, v)
            out = out.transpose(0, 2, 1, 3).reshape(B, T, D)
            return out @ Wo.T + bo
        key = jax.random.key(seed)
        ks = jax.random.split(key, 13)
        s = 0.02
        inp = {'x': jax.random.normal(ks[0], (2, 256, D), dtype=jnp.float32), 'in_proj_w': jax.random.normal(ks[1], (L, 3 * D, D), dtype=jnp.float32) * s, 'in_proj_b': jnp.zeros((L, 3 * D), dtype=jnp.float32), 'out_proj_w': jax.random.normal(ks[2], (L, D, D), dtype=jnp.float32) * s, 'out_proj_b': jnp.zeros((L, D), dtype=jnp.float32), 'ffn1_w': jax.random.normal(ks[3], (L, F, D), dtype=jnp.float32) * s, 'ffn1_b': jnp.zeros((L, F), dtype=jnp.float32), 'ffn2_w': jax.random.normal(ks[4], (L, D, F), dtype=jnp.float32) * s, 'ffn2_b': jnp.zeros((L, D), dtype=jnp.float32), 'ln1_w': jnp.ones((L, D), dtype=jnp.float32), 'ln1_b': jnp.zeros((L, D), dtype=jnp.float32), 'ln2_w': jnp.ones((L, D), dtype=jnp.float32), 'ln2_b': jnp.zeros((L, D), dtype=jnp.float32), 'final_w': jnp.ones((D,), dtype=jnp.float32), 'final_b': jnp.zeros((D,), dtype=jnp.float32)}
        return inp
    _L0_attn_in = _L0_attn_setup()

    def _L0_ffn_setup():
        import jax, jax.numpy as jnp
        import numpy as np
        D_MODEL = 128
        D_FF = 512
        NUM_EXPERTS = 8
        TOP_K = 2
        B, S = (4, 512)
        key = jax.random.key(seed)
        ks = jax.random.split(key, 7)
        s_dm = 1.0 / np.sqrt(D_MODEL)
        s_ff = 1.0 / np.sqrt(D_FF)
        return {'x': jax.random.normal(ks[0], (B, S, D_MODEL), jnp.float32), 'router_w': jax.random.normal(ks[1], (D_MODEL, NUM_EXPERTS), jnp.float32) * s_dm, 'router_b': jnp.zeros((NUM_EXPERTS,), jnp.float32), 'w1': jax.random.normal(ks[2], (NUM_EXPERTS, D_MODEL, D_FF), jnp.float32) * s_dm, 'b1': jnp.zeros((NUM_EXPERTS, D_FF), jnp.float32), 'w2': jax.random.normal(ks[3], (NUM_EXPERTS, D_FF, D_MODEL), jnp.float32) * s_ff, 'b2': jnp.zeros((NUM_EXPERTS, D_MODEL), jnp.float32)}
    _L0_ffn_in = _L0_ffn_setup()
    _d = {'L0_attn_x': _L0_attn_in['x'], 'L0_attn_in_proj_w': _L0_attn_in['in_proj_w'], 'L0_attn_in_proj_b': _L0_attn_in['in_proj_b'], 'L0_attn_out_proj_w': _L0_attn_in['out_proj_w'], 'L0_attn_out_proj_b': _L0_attn_in['out_proj_b'], 'L0_attn_ffn1_w': _L0_attn_in['ffn1_w'], 'L0_attn_ffn1_b': _L0_attn_in['ffn1_b'], 'L0_attn_ffn2_w': _L0_attn_in['ffn2_w'], 'L0_attn_ffn2_b': _L0_attn_in['ffn2_b'], 'L0_attn_ln1_w': _L0_attn_in['ln1_w'], 'L0_attn_ln1_b': _L0_attn_in['ln1_b'], 'L0_attn_ln2_w': _L0_attn_in['ln2_w'], 'L0_attn_ln2_b': _L0_attn_in['ln2_b'], 'L0_attn_final_w': _L0_attn_in['final_w'], 'L0_attn_final_b': _L0_attn_in['final_b'], 'L0_ffn_router_w': _L0_ffn_in['router_w'], 'L0_ffn_router_b': _L0_ffn_in['router_b'], 'L0_ffn_w1': _L0_ffn_in['w1'], 'L0_ffn_b1': _L0_ffn_in['b1'], 'L0_ffn_w2': _L0_ffn_in['w2'], 'L0_ffn_b2': _L0_ffn_in['b2']}
    _x0 = _d['L0_attn_x']
    _d['L0_attn_x'] = jax.random.normal(jax.random.fold_in(jax.random.key(seed), 1), (2, 1024, 128), dtype=_x0.dtype)
    del _x0
    return _d

def reference(L0_attn_x, L0_attn_in_proj_w, L0_attn_in_proj_b, L0_attn_out_proj_w, L0_attn_out_proj_b, L0_attn_ffn1_w, L0_attn_ffn1_b, L0_attn_ffn2_w, L0_attn_ffn2_b, L0_attn_ln1_w, L0_attn_ln1_b, L0_attn_ln2_w, L0_attn_ln2_b, L0_attn_final_w, L0_attn_final_b, L0_ffn_router_w, L0_ffn_router_b, L0_ffn_w1, L0_ffn_b1, L0_ffn_w2, L0_ffn_b2):

    def _L0_attn_ref(x, in_proj_w, in_proj_b, out_proj_w, out_proj_b, ffn1_w, ffn1_b, ffn2_w, ffn2_b, ln1_w, ln1_b, ln2_w, ln2_b, final_w, final_b):
        import math
        import jax, jax.numpy as jnp
        import numpy as np
        L, D, H, F = (4, 128, 16, 512)
        HD = D // H
        EPS = 1e-05

        def get_alibi_slopes(num_heads):
            closest = 2 ** math.floor(math.log2(num_heads))
            base = 2 ** (-2 ** (-(math.log2(closest) - 3)))
            slopes = base ** np.arange(1, closest + 1)
            if closest != num_heads:
                extra_base = 2 ** (-2 ** (-(math.log2(2 * closest) - 3)))
                extra = extra_base ** np.arange(1, 2 * (num_heads - closest) + 1, 2)
                slopes = np.concatenate([slopes, extra])
            return jnp.asarray(slopes, dtype=jnp.float32)

        def build_mask(num_heads, T):
            pos = jnp.arange(T)
            dist = pos[None, :] - pos[:, None]
            alibi = get_alibi_slopes(num_heads)[:, None, None] * dist[None]
            causal = jnp.where(dist > 0, -jnp.inf, 0.0).astype(jnp.float32)
            return causal[None] + alibi

        def layer_norm(x, w, b):
            mu = jnp.mean(x, axis=-1, keepdims=True)
            var = jnp.mean(jnp.square(x - mu), axis=-1, keepdims=True)
            return (x - mu) * jax.lax.rsqrt(var + EPS) * w + b

        def mha(x, mask, Wi, bi, Wo, bo):
            B, T, _ = x.shape
            qkv = x @ Wi.T + bi
            q, k, v = jnp.split(qkv, 3, axis=-1)
            q = q.reshape(B, T, H, HD).transpose(0, 2, 1, 3)
            k = k.reshape(B, T, H, HD).transpose(0, 2, 1, 3)
            v = v.reshape(B, T, H, HD).transpose(0, 2, 1, 3)
            scores = jnp.einsum('bhqd,bhkd->bhqk', q, k) / math.sqrt(HD)
            scores = scores + mask[None]
            attn = jax.nn.softmax(scores, axis=-1)
            out = jnp.einsum('bhqk,bhkd->bhqd', attn, v)
            out = out.transpose(0, 2, 1, 3).reshape(B, T, D)
            return out @ Wo.T + bo
        T = x.shape[1]
        mask = build_mask(H, T)
        for i in range(L):
            xn = layer_norm(x, ln1_w[i], ln1_b[i])
            x = x + mha(xn, mask, in_proj_w[i], in_proj_b[i], out_proj_w[i], out_proj_b[i])
            xn = layer_norm(x, ln2_w[i], ln2_b[i])
            h = jax.nn.gelu(xn @ ffn1_w[i].T + ffn1_b[i], approximate=False)
            x = x + (h @ ffn2_w[i].T + ffn2_b[i])
        return layer_norm(x, final_w, final_b)

    def _L0_ffn_ref(x, router_w, router_b, w1, b1, w2, b2):
        import jax, jax.numpy as jnp
        import numpy as np
        D_MODEL = 128
        D_FF = 512
        NUM_EXPERTS = 8
        TOP_K = 2
        B, S = (4, 512)
        Bx, Sx, D = x.shape
        xf = x.reshape(-1, D)
        logits = xf @ router_w + router_b
        top_w, sel = jax.lax.top_k(logits, TOP_K)
        gates = jax.nn.softmax(top_w, axis=-1)

        def body(i, acc):
            h = jax.nn.gelu(xf @ w1[i] + b1[i], approximate=False)
            out_i = h @ w2[i] + b2[i]
            gate_i = jnp.sum(gates * (sel == i), axis=-1, keepdims=True)
            return acc + out_i * gate_i
        out = jax.lax.fori_loop(0, NUM_EXPERTS, body, jnp.zeros_like(xf))
        return out.reshape(Bx, Sx, D)
    x = L0_attn_x
    xn = _layernorm(x, axis=-1)
    x = x + _L0_attn_ref(xn, L0_attn_in_proj_w, L0_attn_in_proj_b, L0_attn_out_proj_w, L0_attn_out_proj_b, L0_attn_ffn1_w, L0_attn_ffn1_b, L0_attn_ffn2_w, L0_attn_ffn2_b, L0_attn_ln1_w, L0_attn_ln1_b, L0_attn_ln2_w, L0_attn_ln2_b, L0_attn_final_w, L0_attn_final_b) + _L0_ffn_ref(xn, L0_ffn_router_w, L0_ffn_router_b, L0_ffn_w1, L0_ffn_b1, L0_ffn_w2, L0_ffn_b2)
    return x

_drawn_inputs = setup_inputs


def setup_inputs(seed=0):
    import zlib

    import numpy as np

    out = dict(_drawn_inputs(seed))
    spreads = {'L0_attn_in_proj_b': (0.0, 0.353),
     'L0_attn_out_proj_b': (0.0, 0.1),
     'L0_attn_ffn1_b': (0.0, 0.323),
     'L0_attn_ffn2_b': (0.0, 0.1),
     'L0_attn_ln1_w': (1.0, 0.6),
     'L0_attn_ln1_b': (0.0, 0.8),
     'L0_attn_ln2_w': (1.0, 0.6),
     'L0_attn_ln2_b': (0.0, 0.8),
     'L0_attn_final_w': (1.0, 0.2),
     'L0_attn_final_b': (0.0, 0.1),
     'L0_ffn_router_b': (0.0, 0.1),
     'L0_ffn_b1': (0.0, 0.329),
     'L0_ffn_b2': (0.0, 0.1)}
    factors = {'L0_attn_in_proj_w': 3.297}
    for name, (base, spread) in spreads.items():
        noise = np.random.default_rng([zlib.crc32(name.encode()), seed]).standard_normal(out[name].shape)
        drawn = base * np.exp(spread * noise) if base else spread * noise
        out[name] = jnp.asarray(drawn.astype(out[name].dtype))
    for name, factor in factors.items():
        out[name] = (out[name] * factor).astype(out[name].dtype)
    return out
```

```python
from contextlib import ExitStack

import concourse.bass as bass
from concourse import mybir

F32 = mybir.dt.float32
BF16 = mybir.dt.bfloat16
U32 = mybir.dt.uint32
ALU = mybir.AluOpType
ACT = mybir.ActivationFunctionType
AXX = mybir.AxisListType.X
ds = bass.ds

B, T, D, L, H, F, E = 2, 1024, 128, 4, 16, 512, 8
P = 128
HD = D // H
NT = B * T // P
TB = T // P
G = 4
UN = B * H // G
FT = F // P
ROWS = 64
MROW = 56
EPS = 1e-5
QSCALE = float(HD) ** -0.5
Q_PARTS = (0, 0, 1, 0, 2, 1)
K_PARTS = (0, 1, 0, 2, 0, 1)

P1_GROUPS = []
for _i in range(TB):
    for _c in range(1 if _i < 4 else 2):
        P1_GROUPS.append((_i, _c, 512 * _c, min(512, P * (_i + 1) - 512 * _c)))
P1N = G * len(P1_GROUPS)
T_AFTER = 3
P2_JOBS = [(qh, kt, max(512 * qh, P * kt), 512 * (qh + 1) - max(512 * qh, P * kt))
           for qh in range(2) for kt in range(4 * (qh + 1))]
JOBN = len(P2_JOBS)
JOB_AFTER = (3, 4, 4, 5, 6, 6, 7, 8, 8, 9, 10, 11)
CH = 12

def p1_places(with_turn):
    places = {}
    pos = 0
    for g in range(len(P1_GROUPS)):
        if with_turn and g == T_AFTER:
            places["turn"] = pos
            pos += 1
        for h in range(G):
            places[G * g + h] = pos
            pos += 1
    return places


def build(nc, x, cA, rA, cB, moe, router_w, rb_b2, fin, ident, identb, iota, m1, m2, kcon, qcon, out):
    with ExitStack() as ctx:
        def sb(name, shape, dt=F32):
            return ctx.enter_context(nc.sbuf_tensor(name, shape, dt))

        def sem(name):
            return ctx.enter_context(nc.semaphore(name))

        def dram(name, shape, dt=F32):
            return nc.dram_tensor(name, shape, dt, kind="Internal").ap()

        PS = ctx.enter_context(nc.psum_tensor("PS", [P, 8, 512], F32))

        kst = dram("kst", [B, H, ROWS, T], BF16)
        qst = dram("qst", [B, H, ROWS, T], BF16)
        onum = dram("onum", [UN, G * HD, T])
        oden = dram("oden", [UN * G, T])
        orec = dram("orec", [UN * G, T])

        idf = sb("idf", [P, P])
        idb = sb("idb", [P, P], BF16)
        io8 = sb("io8", [P, E])
        mk1 = sb("mk1", [P, 2, P], BF16)
        mk2 = sb("mk2", [P, 2, P], BF16)
        mhalf = sb("mhalf", [P, TB])
        rw = sb("rw", [P, E])
        rb = sb("rb", [P, E])
        b2e = sb("b2e", [E, D])
        finw = sb("finw", [P, 2, D])
        wA = sb("wA", [P, 3 * D + 4])
        wV = sb("wV", [P, D])
        wR = sb("wR", [P, 2, D])
        wB = sb("wB", [P, D + 2])
        NW = 2 * F + FT
        wE = [sb(f"wE{i}", [P, NW]) for i in range(3)]
        xin = sb("xin", [P, NT, D])
        xr = sb("xr", [P, NT, D])
        acc = sb("acc", [P, NT, D])
        xc = sb("xc", [P, NT, D])
        xn0T = sb("xn0T", [P, B, T])
        xnT = sb("xnT", [P, B, T])
        st = sb("st", [P, 2, TB, 6])
        mv = sb("mv", [P, 2, TB, 2])
        ve = sb("ve", [P, 2, TB])
        rstd = sb("rstd", [P, 2, TB])
        lg = sb("lg", [P, NT, E])
        v8 = sb("v8", [P, NT, E])
        i8 = sb("i8", [P, NT, E], U32)
        i8f = sb("i8f", [P, NT, E])
        gd = sb("gd", [P, NT])
        ge = sb("ge", [P, NT])
        g1 = sb("g1", [P, NT])
        g2 = sb("g2", [P, NT])
        eq = sb("eq", [P, 2, NT, E])
        gate = sb("gate", [P, NT, E])
        gT = sb("gT", [E, NT * P])
        x32 = sb("x32", [P, B, 2, T])
        OT = x32[:, :, 0, :]
        rT = x32[:, :, 1, :]
        parts = sb("parts", [P, 3, B, 2, T], BF16)
        vsb = sb("vsb", [P, UN, TB, G * HD])
        vbuf = sb("vbuf", [P, 2, TB, G, 32])
        Kop = sb("Kop", [P, 2, 2, T], BF16)
        Qop = sb("Qop", [P, 2, 2, T], BF16)
        mx = sb("mx", [P, 2, TB, G, 2])
        negm = sb("negm", [P, 2, TB, G])
        mres = sb("mres", [P, 2, TB, G])
        mp = sb("mp", [P, 2, TB, G, 3], BF16)
        mrow = sb("mrow", [G * 3, 2, T], BF16)
        PR = sb("PR", [P, 4, 2, 512])
        osb = sb("osb", [P, 2, 512])
        den = sb("den", [P, 2, P])
        hb = sb("hb", [P, 2, FT, 512])
        gcur = sb("gcur", [P, 2, NT])

        names = """c_const c_x c_wA c_wB c_stg0 c_stg1 c_con c_den c_rec c_OT c_out
            s_lnst s_lnag s_lnve s_lnrs s_lnxc s_lnT s_lnev
            s_ms s_lgp s_lg s_v8 s_i8 s_gd s_ge s_g s_gate s_gTp s_gT s_a0p s_a0
            s_qk s_q32 s_v s_vev s_hi s_r s_mid s_lo s_bias
            s_p1 s_p1m s_negm s_mpool s_turn s_mrow s_vb
            s_s2 s_exp s_pv s_oev s_rc s_onT s_wo s_woev
            s_h s_gelu s_y s_yev s_fin""".split()
        S = {n: sem(n) for n in names}
        c_ldl = [sem(f"c_ldl{i}") for i in range(2)]
        c_ldr = [sem(f"c_ldr{i}") for i in range(2)]
        c_m = [sem(f"c_m{i}") for i in range(2)]
        c_o = [sem(f"c_o{i}") for i in range(2)]
        s_gc = sem("s_gc")
        passed = sem("passed")
        c_stg = [S["c_stg0"], S["c_stg1"]]
        ODMA = 16 * 5
        CR_EXP, CR_PV, CR_OEV, CR_GELU, CR_Y, CR_YEV, CR_M = 2, 2, 1, 4, 2, 4, 1

        block = ctx.enter_context(nc.Block())
        kcov = kcon.bitcast(BF16).rearrange("h r t -> h (r t)")
        qcov = qcon.bitcast(BF16).rearrange("h r t -> h (r t)")
        xv = x.rearrange("b (t p) d -> p (b t) d", p=P)
        ov = out.rearrange("b (t p) d -> p (b t) d", p=P)
        kun = kst.rearrange("b (g a j) r t -> (b g) (j r) a t", a=2, j=2)
        qun = qst.rearrange("b (g a j) r t -> (b g) (j r) a t", a=2, j=2)

        stage_places, first_places = p1_places(True), p1_places(False)
        turn_bank = 5 + stage_places["turn"] % 3
        TURN = PS[:, turn_bank, :].bitcast(BF16)[0:3 * G, :]

        def wait_apart(eng, semaphore, value):
            eng.wait_ge(semaphore, value)
            eng.sem_inc(passed, 1)

        @block.sync
        def _(sp):
            for h in range(2):
                sp.dma_start(xin[:, TB * h:TB * h + TB, :], xv[:, TB * h:TB * h + TB, :]).then_inc(S["c_x"], 16)
            for dst, src in ((idf[:, :], ident), (idb[:, :], identb.bitcast(BF16)), (io8[:, :], iota), (mk1[:, :, :], m1.bitcast(BF16)),
                             (mk2[:, :, :], m2.bitcast(BF16)), (rw[:, :], router_w),
                             (rb[:, :], rb_b2[0:1, 0:E].to_broadcast([P, E])),
                             (b2e[:, :], rb_b2[1:1 + E, :]),
                             (finw[:, :, :], fin.unsqueeze(0).to_broadcast([P, 2, D]))):
                sp.dma_start(dst, src).then_inc(S["c_const"], 16)
            for b in range(B):
                for dst, src in ((kst, kcov), (qst, qcov)):
                    sp.dma_start(dst[b, :, 6 * HD:ROWS, :].rearrange("h r t -> h (r t)"), src)\
                        .then_inc(S["c_con"], 16)
            sp.wait_ge(S["c_con"], 64)

            def load(u, U, par, half):
                c = (c_ldl, c_ldr)[half][par]
                cols = slice(512 * half, 512 * half + 512)
                sp.dma_start(Qop[:, par, :, cols], qun[ds(u, 1), :, :, cols].rearrange("u p a t -> (u p) a t"))\
                    .then_inc(c, 16)
                sp.dma_start(Kop[:, par, :, cols], kun[ds(u, 1), :, :, cols].rearrange("u p a t -> (u p) a t"))\
                    .then_inc(c, 16)

            def minus_max(U, par):
                sp.wait_ge(S["s_mrow"], U + 1 + CR_M)
                for h in range(G):
                    sp.dma_start(Qop[64 * (h % 2) + MROW:64 * (h % 2) + MROW + 3, par, h // 2, :],
                                 mrow[3 * h:3 * h + 3, par, :]).then_inc(c_m[par], 16)

            def outputs(u, U, qh):
                sp.wait_ge(S["s_oev"], 2 * U + qh + 1 + CR_OEV)
                cols = slice(512 * qh, 512 * qh + 512)
                for h in range(G):
                    sp.dma_start(onum[ds(u, 1), HD * h:HD * h + HD, cols].rearrange("u r t -> (u r) t"),
                                 osb[32 * h:32 * h + HD, qh, :]).then_inc(c_o[qh], 16)
                sp.dma_start(oden[ds(G * u, G), cols], osb[HD:P:32, qh, :]).then_inc(c_o[qh], 16)

            def stage(l, u, par, more):
                U = 8 * l + u
                minus_max(U, par)
                outputs(u, U, 0)
                if more:
                    sp.wait_ge(S["s_s2"], 24 * U + 16)
                    load(u + 2, U, par, 0)
                    sp.wait_ge(S["s_s2"], 24 * U + 24)
                    load(u + 2, U, par, 1)
                outputs(u, U, 1)

            with sp.Fori(0, L, 1) as l:
                sp.dma_start(wA[:, :], cA[ds(l, 1), :, :].rearrange("l p n -> (l p) n")).then_inc(S["c_wA"], 16)
                sp.dma_start(wV[:, :], rA[ds(l, 1), 0, :].to_broadcast([P, D])).then_inc(S["c_wA"], 16)
                for e in range(2):
                    sp.dma_start(wE[e][:, :], moe[ds(2 * l + e, 1), :, :].rearrange("l p n -> (l p) n"))\
                        .then_inc(S["c_wA"], 16)
                for b in range(B):
                    for s, stg, which in ((0, qst, Q_PARTS), (1, kst, K_PARTS)):
                        for part, done in ((0, "s_hi"), (1, "s_mid"), (2, "s_lo")):
                            sp.wait_ge(S[done], 4 * l + 2 * b + s + 1)
                            for blk in range(6):
                                if which[blk] == part:
                                    sp.dma_start(stg[b, :, HD * blk:HD * blk + HD, :], parts[:, part, b, s, :])\
                                        .then_inc(c_stg[b], 16)
                    wait_apart(sp, c_stg[b], 192 * (l + 1))
                    if b == 0:
                        for u in range(2):
                            for half in range(2):
                                load(u, 8 * l + u, u, half)
                        sp.dma_start(wB[:, :], cB[ds(l, 1), :, NW:]
                                     .rearrange("l p n -> (l p) n")).then_inc(S["c_wB"], 16)
                        sp.dma_start(wE[2][:, :], cB[ds(l, 1), :, 0:NW]
                                     .rearrange("l p n -> (l p) n")).then_inc(S["c_wB"], 16)
                        sp.dma_start(wR[:, :, :], rA[ds(l, 1), 1:3, :].to_broadcast([P, 2, D]))\
                            .then_inc(S["c_wB"], 16)
                with sp.Fori(0, UN // 2 - 1, 1) as i:
                    stage(l, 2 * i, 0, True)
                    stage(l, 2 * i + 1, 1, True)
                stage(l, UN - 2, 0, False)
                stage(l, UN - 1, 1, False)
                for qh in range(2):
                    sp.wait_ge(c_o[qh], ODMA * (8 * l + 8) + ODMA)
                for b in range(B):
                    rows = slice(UN * G // 2 * b, UN * G // 2 * (b + 1))
                    sp.dma_start(den[:, b, :], oden[rows, :].rearrange("h (c n) -> (h c) n", n=P))\
                        .then_inc(S["c_den"], 16)
                    sp.dma_start(OT[:, b, :], onum[4 * b:4 * b + 4, :, :].rearrange("u r t -> (u r) t"))\
                        .then_inc(S["c_OT"], 16)
                for b in range(B):
                    rows = slice(UN * G // 2 * b, UN * G // 2 * (b + 1))
                    sp.wait_ge(S["s_rc"], 2 * l + b + 1)
                    sp.dma_start(orec[rows, :].rearrange("h (c n) -> (h c) n", n=P), den[:, b, :])\
                        .then_inc(S["c_rec"], 16)
                sp.wait_ge(S["c_rec"], 32 * l + 32)
                for b in range(B):
                    rows = slice(UN * G // 2 * b, UN * G // 2 * (b + 1))
                    sp.dma_start(rT[:, b, :], orec[rows, :].unsqueeze(1).to_broadcast([H, HD, T]))\
                        .then_inc(S["c_OT"], 16)
            for h in range(2):
                sp.wait_ge(S["s_fin"], 4 * h + 4)
                sp.dma_start(ov[:, TB * h:TB * h + TB, :], xc[:, TB * h:TB * h + TB, :]).then_inc(S["c_out"], 16)
            sp.wait_ge(S["c_out"], 32)

        @block.gpsimd
        def _(pool):
            pool.memset(mhalf[:, :], -0.5).then_inc(S["s_ms"], 1)
            pool.memset(vbuf[:, :, :, :, :], 1.0).then_inc(S["s_ms"], 1)
            pool.memset(mx[:, :, :, :, :], -3.0e38).then_inc(S["s_ms"], 1)
            pool.wait_ge(S["s_ms"], 3)

            def rstd_of(idx, h):
                pool.wait_ge(S["s_lnve"], idx + 1)
                pool.tensor_tensor(rstd[:, h, :], ve[:, h, :], mhalf[:, :], ALU.pow).then_inc(S["s_lnrs"], 1)

            def split(l, b, s):
                n = 4 * l + 2 * b + s
                pool.wait_ge(S["s_hi"], n + 1)
                pool.tensor_tensor(x32[:, b, s, :], x32[:, b, s, :], parts[:, 0, b, s, :], ALU.subtract)\
                    .then_inc(S["s_r"], 1)
                pool.wait_ge(S["s_mid"], n + 1)
                pool.tensor_tensor(parts[:, 2, b, s, :], x32[:, b, s, :], parts[:, 1, b, s, :], ALU.subtract)\
                    .then_inc(S["s_lo"], 1)

            def add_bias(row):
                pool.tensor_tensor(xr[:, :, :], xr[:, :, :], wR[:, row:row + 1, :].to_broadcast([P, NT, D]), ALU.add)\
                    .then_inc(S["s_bias"], 1)

            def values(u, par):
                pool.tensor_copy(vbuf[:, par, :, :, 0:HD],
                                 vsb[:, ds(u, 1), :, :].rearrange("p u k (g e) -> p (u k) g e", g=G))\
                    .then_inc(S["s_vb"], 1)

            def max_parts(U, par):
                wait_apart(pool, S["s_negm"], U + 1)
                pool.tensor_copy(mp[:, par, :, :, 0], negm[:, par, :, :]).then_inc(S["s_mpool"], 1)
                pool.wait_ge(S["s_mpool"], 4 * U + 1)
                pool.tensor_tensor(mres[:, par, :, :], negm[:, par, :, :], mp[:, par, :, :, 0], ALU.subtract)\
                    .then_inc(S["s_mpool"], 1)
                wait_apart(pool, S["s_mpool"], 4 * U + 2)
                pool.tensor_copy(mp[:, par, :, :, 1], mres[:, par, :, :]).then_inc(S["s_mpool"], 1)
                pool.wait_ge(S["s_mpool"], 4 * U + 3)
                pool.tensor_tensor(mp[:, par, :, :, 2], mres[:, par, :, :], mp[:, par, :, :, 1], ALU.subtract)\
                    .then_inc(S["s_mpool"], 1)

            def stage(l, u, par):
                U = 8 * l + u
                wait_apart(pool, S["s_pv"], 12 * U + CR_PV)
                values(u + 1, 1 - par)
                max_parts(U + 1, 1 - par)

            for h in range(2):
                rstd_of(h, h)
            with pool.Fori(0, L, 1) as l:
                for h in range(2):
                    rstd_of(4 * l + 2 + h, h)
                for b in range(B):
                    for s in range(2):
                        split(l, b, s)
                wait_apart(pool, S["s_vev"], 2 * l + 2)
                values(0, 0)
                max_parts(8 * l, 0)
                pool.wait_ge(S["c_wB"], 48 * (l + 1))
                pool.wait_ge(S["s_lnxc"], 4 * l + 4)
                add_bias(0)
                with pool.Fori(0, UN // 2 - 1, 1) as i:
                    stage(l, 2 * i, 0)
                    stage(l, 2 * i + 1, 1)
                stage(l, UN - 2, 0)
                for h in range(2):
                    rstd_of(4 * l + 4 + h, h)
                pool.wait_ge(S["s_lnxc"], 4 * l + 6)
                add_bias(1)
            for h in range(2):
                rstd_of(4 * L + 2 + h, h)

        @block.scalar
        def _(act):
            act.sem_inc(S["s_exp"], CR_EXP)
            act.sem_inc(S["s_oev"], CR_OEV)
            act.sem_inc(S["s_gelu"], CR_GELU)
            act.sem_inc(S["s_mrow"], CR_M)

            def ln_out(idx, h, dst, w):
                act.wait_ge(S["s_lnT"], idx + 1)
                src = PS[:, 4 + 2 * h:6 + 2 * h, :]
                if w is None:
                    act.activation(dst[:, h, :], src, ACT.Copy).then_inc(S["s_lnev"], 1)
                else:
                    act.activation(dst[:, h, :], src, ACT.Identity, scale=w[0], bias=w[1]).then_inc(S["s_lnev"], 1)

            def gelu(l, c):
                m = CH * l + c
                for f in range(FT):
                    act.wait_ge(S["s_h"], 4 * m + f + 1)
                    if f == 0:
                        act.wait_ge(S["s_y"], m - 1 + CR_Y)
                    act.activation(hb[:, c % 2, f, :], PS[:, f, :], ACT.Gelu,
                                   bias=wE[c // 4][:, 2 * F + f:2 * F + f + 1]).then_inc(S["s_gelu"], 1)

            def turn_out(U, par):
                act.wait_ge(S["s_turn"], U + 1)
                act.activation(mrow[:, par, :], TURN, ACT.Copy).then_inc(S["s_mrow"], 1)

            def exps(U, t):
                n = P2_JOBS[t][3]
                for a in range(2):
                    c = 2 * t + a
                    act.wait_ge(S["s_s2"], 24 * U + c + 1)
                    if a == 0:
                        act.wait_ge(S["s_pv"], 12 * U + t - 1 + CR_PV)
                    act.activation(PR[:, 2 * (t % 2) + a, :, 0:n], PS[:, 2 * (c % 2):2 * (c % 2) + 2, 0:n], ACT.Exp)\
                        .then_inc(S["s_exp"], 1)

            def sums_out(U, qh):
                act.wait_ge(S["s_pv"], 12 * U + (4, 12)[qh] + CR_PV)
                act.wait_ge(c_o[qh], ODMA * U + ODMA)
                act.activation(osb[:, qh, :], PS[:, 4, :], ACT.Copy).then_inc(S["s_oev"], 1)

            def stage(l, u, par):
                U = 8 * l + u
                turn_out(U, par)
                for t in range(JOBN):
                    exps(U, t)
                    if t == 5:
                        sums_out(U, 0)
                sums_out(U, 1)

            for h in range(2):
                ln_out(h, h, xn0T, None)
            act.wait_ge(S["s_gd"], 1)
            act.activation(ge[:, :], gd[:, :], ACT.Exp).then_inc(S["s_ge"], 1)
            act.wait_ge(S["s_gTp"], 1)
            act.activation(gT[:, :], PS[0:E, 4:8, :], ACT.Copy).then_inc(S["s_gT"], 1)
            with act.Fori(0, L, 1) as l:
                act.wait_ge(S["c_wA"], 64 * (l + 1))
                for h in range(2):
                    ln_out(4 * l + 2 + h, h, xnT, (wA[:, 3 * D:3 * D + 1], wA[:, 3 * D + 1:3 * D + 2]))
                for b in range(B):
                    for s in range(2):
                        n = 4 * l + 2 * b + s
                        act.wait_ge(S["s_q32"], n + 1)
                        act.activation(parts[:, 0, b, s, :], x32[:, b, s, :], ACT.Copy).then_inc(S["s_hi"], 1)
                        act.wait_ge(S["s_r"], n + 1)
                        act.activation(parts[:, 1, b, s, :], x32[:, b, s, :], ACT.Copy).then_inc(S["s_mid"], 1)
                for c in range(8):
                    gelu(l, c)
                with act.Fori(0, UN // 2 - 1, 1) as i:
                    stage(l, 2 * i, 0)
                    stage(l, 2 * i + 1, 1)
                stage(l, UN - 2, 0)
                stage(l, UN - 1, 1)
                act.wait_ge(S["c_wB"], 48 * (l + 1))
                for h in range(2):
                    ln_out(4 * l + 4 + h, h, xnT, (wB[:, D:D + 1], wB[:, D + 1:D + 2]))
                for c in range(8, 12):
                    gelu(l, c)


        @block.tensor
        def _(pe):
            pe.sem_inc(S["s_pv"], CR_PV)
            pe.sem_inc(S["s_y"], CR_Y)

            def ln_turn(idx, h, src):
                pe.wait_ge(S["s_lnxc"], idx + 1)
                for t in range(TB):
                    last = pe.transpose(PS[:, 4 + 2 * h + t // 4, P * (t % 4):P * (t % 4) + P], src[:, TB * h + t, :],
                                        idf[:, :])
                last.then_inc(S["s_lnT"], 1)

            def expert_h(l, c, src):
                m = CH * l + c
                w = wE[c // 4]
                tok = src[:, (c % 4) // 2, 512 * (c % 2):512 * (c % 2) + 512]
                for f in range(FT):
                    pe.wait_ge(S["s_gelu"], 4 * m - 4 + f + 1 + CR_GELU)
                    pe.matmul(PS[:, f, :], w[:, P * f:P * f + P], tok, start=True, stop=True).then_inc(S["s_h"], 1)

            def expert_y(l, c):
                m = CH * l + c
                w = wE[c // 4]
                pe.wait_ge(S["s_gelu"], 4 * m + 4 + CR_GELU)
                pe.wait_ge(S["s_yev"], m + CR_YEV)
                for j in range(4):
                    for f in range(FT):
                        last = pe.matmul(PS[:, 4, P * j:P * j + P], hb[:, c % 2, f, P * j:P * j + P],
                                         w[:, F + P * f:F + P * f + P], start=(f == 0), stop=(f == FT - 1))
                last.then_inc(S["s_y"], 1)

            def p1_group(U, par, g, places):
                i, c, k0, n = P1_GROUPS[g]
                diag = P * i >= k0 and P * i < k0 + n
                for h in range(G):
                    k = G * g + h
                    pos = places[k]
                    if pos >= 3:
                        before = next(q for q, p in places.items() if p == pos - 3)
                        if before == "turn":
                            pe.wait_ge(S["s_mrow"], U - 1 + 1 + CR_M)
                        else:
                            pe.wait_ge(S["s_p1m"], P1N * U + before + 1)
                    elif "turn" in places:
                        pe.wait_ge(S["s_negm"], U)
                    a, j = h // 2, h % 2
                    bank = 5 + pos % 3
                    r = slice(ROWS * j, ROWS * j + MROW)
                    rr = slice(ROWS * j, ROWS * j + ROWS)
                    last = pe.matmul(PS[:, bank, 0:n], Qop[r, par, a, P * i:P * i + P], Kop[r, par, a, k0:k0 + n],
                                     start=True, stop=not diag)
                    if diag:
                        for cc in range(2):
                            o = n - P + 64 * cc
                            last = pe.matmul(PS[:, bank, o:o + 64], mk1[rr, cc, :], idb[rr, rr],
                                             start=False, stop=(cc == 1))
                    last.then_inc(S["s_p1"], 1)

            def operands(n, par, half):
                pe.wait_ge((c_ldl, c_ldr)[half][par], 32 * (n + 1))

            def turn(U, par, more):
                pe.wait_ge(S["s_mpool"], 4 * U + 4)
                if more:
                    pe.wait_ge(S["s_p1m"], P1N * U + P1N + 1 +
                               next(k for k, p in stage_places.items() if p == stage_places["turn"] - 3))
                for i in range(TB):
                    last = pe.transpose(TURN[:, P * i:P * i + P],
                                        mp[:, par, i, :, :].rearrange("p g c -> p (g c)"), idb[:, :])
                last.then_inc(S["s_turn"], 1)

            def p2_scores(U, par, t):
                qh, kt, q0, n = P2_JOBS[t]
                for a in range(2):
                    c = 2 * t + a
                    pe.wait_ge(S["s_exp"], 24 * U + c - 1 + CR_EXP)
                    diag = P * kt >= 512 * qh
                    for j in range(2):
                        rr = slice(ROWS * j, ROWS * j + ROWS)
                        last = pe.matmul(PS[:, 2 * (c % 2) + j, 0:n], Kop[rr, par, a, P * kt:P * kt + P],
                                         Qop[rr, par, a, q0:q0 + n], start=True, stop=not diag)
                    if diag:
                        for cc in range(2):
                            for j in range(2):
                                rr = slice(ROWS * j, ROWS * j + ROWS)
                                last = pe.matmul(PS[:, 2 * (c % 2) + j, 64 * cc:64 * cc + 64], mk2[rr, cc, :],
                                                 idb[rr, rr], start=False, stop=(cc == 1))
                    last.then_inc(S["s_s2"], 1)

            def p2_values(U, par, t):
                qh, kt, q0, n = P2_JOBS[t]
                if t == 0:
                    pe.wait_ge(S["s_vb"], U + 1)
                if kt == 0:
                    pe.wait_ge(S["s_oev"], 2 * U + qh + CR_OEV)
                pe.wait_ge(S["s_exp"], 24 * U + 2 * t + 2 + CR_EXP)
                for h in range(G):
                    last = pe.matmul(PS[32 * h:32 * h + 32, 4, q0 - 512 * qh:512], vbuf[:, par, kt, h, :],
                                     PR[:, 2 * (t % 2) + h // 2, h % 2, 0:n],
                                     start=(kt == 0), stop=(kt == 4 * qh + 3))
                last.then_inc(S["s_pv"], 1)

            def stage(l, u, par, nth, more):
                U = 8 * l + u
                nxt = nth + par
                def jobs(g):
                    for t in range(JOBN):
                        if JOB_AFTER[t] == g:
                            if t == 0:
                                pe.wait_ge(c_m[par], 64 * (nth + 1))
                            p2_scores(U, par, t)
                            if t >= 1:
                                p2_values(U, par, t - 1)
                for g in range(len(P1_GROUPS)):
                    if g == T_AFTER:
                        turn(U, par, more)
                    if more:
                        if g == 0:
                            operands(nxt, 1 - par, 0)
                        if g == 4:
                            operands(nxt, 1 - par, 1)
                        p1_group(U + 1, 1 - par, g, stage_places)
                    jobs(g)
                p2_values(U, par, JOBN - 1)

            pe.wait_ge(S["c_const"], 16 * 9)
            for h in range(2):
                ln_turn(h, h, xr)
            pe.wait_ge(S["s_lnev"], 2)
            for t in range(NT):
                last = pe.matmul(PS[:, 4, E * t:E * t + E], xn0T[:, t // TB, P * (t % TB):P * (t % TB) + P], rw[:, :],
                                 start=True, stop=True)
            last.then_inc(S["s_lgp"], 1)
            pe.wait_ge(S["s_gate"], 1)
            for t in range(NT):
                last = pe.transpose(PS[0:E, 4 + t // 4, P * (t % 4):P * (t % 4) + P], gate[:, t, :], idf[:, :])
            last.then_inc(S["s_gTp"], 1)
            pe.wait_ge(S["s_gT"], 1)
            for t in range(NT):
                last = pe.matmul(PS[:, t // 4, P * (t % 4):P * (t % 4) + P], gT[:, P * t:P * t + P], b2e[:, :],
                                 start=True, stop=True)
            last.then_inc(S["s_a0p"], 1)
            pe.wait_ge(S["s_a0"], 1)

            with pe.Fori(0, L, 1) as l:
                for h in range(2):
                    ln_turn(4 * l + 2 + h, h, xc)
                pe.wait_ge(S["c_wA"], 64 * (l + 1))
                for b in range(B):
                    pe.wait_ge(S["s_lnev"], 4 * l + 3 + b)
                    for s in range(2):
                        if b == 1:
                            pe.wait_ge(S["s_q32"], 4 * l + s + 1)
                        for n in range(2):
                            last = pe.matmul(PS[:, 2 * s + n, :], wA[:, D * s:D * s + D],
                                             xnT[:, b, 512 * n:512 * n + 512], start=True, stop=True)
                        last.then_inc(S["s_qk"], 1)
                    for t in range(TB):
                        last = pe.matmul(PS[:, 4 + 2 * b + t // 4, P * (t % 4):P * (t % 4) + P],
                                         xnT[:, b, P * t:P * t + P], wA[:, 2 * D:3 * D], start=True, stop=True)
                    last.then_inc(S["s_v"], 1)
                pe.wait_ge(S["s_vev"], 2 * l + 2)
                pe.wait_ge(S["s_q32"], 4 * l + 4)
                expert_h(l, 0, xn0T)
                for c in range(1, 4):
                    expert_h(l, c, xn0T)
                    expert_y(l, c - 1)
                operands(4 * l, 0, 0)
                for c in range(4, 8):
                    expert_h(l, c, xn0T)
                    for g in range(3 * (c - 4), 3 * (c - 4) + 3):
                        if g == 4:
                            operands(4 * l, 0, 1)
                        p1_group(8 * l, 0, g, first_places)
                    expert_y(l, c - 1)
                expert_y(l, 7)
                wait_apart(pe, S["s_yev"], 12 * l + 8 + CR_YEV)
                with pe.Fori(0, UN // 2 - 1, 1) as i:
                    stage(l, 2 * i, 0, 4 * l + i, True)
                    stage(l, 2 * i + 1, 1, 4 * l + i, True)
                stage(l, UN - 2, 0, 4 * l + 3, True)
                stage(l, UN - 1, 1, 4 * l + 3, False)
                pe.wait_ge(S["s_oev"], 16 * l + 16 + CR_OEV)
                pe.wait_ge(S["c_wB"], 48 * (l + 1))
                for b in range(B):
                    pe.wait_ge(S["s_onT"], 2 * l + b + 1)
                    for t in range(TB):
                        last = pe.matmul(PS[:, 2 * b + t // 4, P * (t % 4):P * (t % 4) + P],
                                         OT[:, b, P * t:P * t + P], wB[:, 0:D], start=True, stop=True)
                    last.then_inc(S["s_wo"], 1)
                for h in range(2):
                    ln_turn(4 * l + 4 + h, h, xc)
                pe.wait_ge(S["s_lnev"], 4 * l + 5)
                expert_h(l, 8, xnT)
                for c in range(9, 12):
                    if c == 10:
                        pe.wait_ge(S["s_lnev"], 4 * l + 6)
                    expert_h(l, c, xnT)
                    expert_y(l, c - 1)
                expert_y(l, 11)

        @block.vector
        def _(dve):
            dve.sem_inc(S["s_yev"], CR_YEV)
            for qh in range(2):
                dve.sem_inc(c_o[qh], ODMA)

            def ln_stats(idx, h, src, dst):
                for t in range(TB):
                    last = dve.bn_stats(st[:, h, t, :], src[:, TB * h + t, :])
                last.then_inc(S["s_lnst"], 1)
                wait_apart(dve, S["s_lnst"], idx + 1)
                for t in range(TB):
                    last = dve.bn_aggr(mv[:, h, t, :], st[:, h, t, :])
                last.then_inc(S["s_lnag"], 1)
                dve.wait_ge(S["s_lnag"], idx + 1)
                dve.tensor_scalar(ve[:, h, :], mv[:, h, :, 1], EPS, None, ALU.add).then_inc(S["s_lnve"], 1)

            def ln_apply(idx, h, src, dst):
                dve.wait_ge(S["s_lnrs"], idx + 1)
                for t in range(TB):
                    last = dve.tensor_scalar(dst[:, TB * h + t, :], src[:, TB * h + t, :], mv[:, h, t, 0:1],
                                             rstd[:, h, t:t + 1], ALU.subtract, ALU.mult)
                last.then_inc(S["s_lnxc"], 1)

            def expert_out(l, c):
                m = CH * l + c
                dve.wait_ge(S["s_y"], m + 1 + CR_Y)
                if c < 8:
                    dve.wait_ge(S["s_yev"], m - 3 + CR_YEV)
                    for j in range(4):
                        t = 4 * (c % 4) + j
                        last = dve.scalar_tensor_tensor(out=acc[:, t, :], in0=PS[:, 4, P * j:P * j + P],
                                                        scalar=gcur[:, c // 4, t:t + 1], in1=acc[:, t, :],
                                                        op0=ALU.mult, op1=ALU.add)
                else:
                    t = 4 * (c % 4)
                    last = dve.tensor_tensor(xr[:, t:t + 4, :], PS[:, 4, :].rearrange("p (t d) -> p t d", t=4),
                                             xr[:, t:t + 4, :], ALU.add)
                last.then_inc(S["s_yev"], 1)

            def maxima(U, par, g):
                i, c, k0, n = P1_GROUPS[g]
                for h in range(G):
                    k = G * g + h
                    dve.wait_ge(S["s_p1"], P1N * U + k + 1)
                    bank = 5 + places[k] % 3
                    dve.tensor_reduce(mx[:, par, i, h, c:c + 1], PS[:, bank, 0:n], AXX, ALU.max)\
                        .then_inc(S["s_p1m"], 1)

            def neg_max(U, par):
                dve.wait_ge(S["s_p1m"], P1N * U + P1N)
                dve.tensor_reduce(negm[:, par, :, :], mx[:, par, :, :, :], AXX, ALU.max, negate=True)\
                    .then_inc(S["s_negm"], 1)

            for h in range(2):
                dve.wait_ge(S["c_x"], 16 * 2)
                ln_stats(h, h, xin, xr)
                ln_apply(h, h, xin, xr)
            dve.wait_ge(S["c_const"], 16 * 9)
            dve.wait_ge(S["s_lgp"], 1)
            dve.tensor_tensor(lg[:, :, :], PS[:, 4, 0:NT * E].rearrange("p (t e) -> p t e", e=E),
                              rb[:, :].unsqueeze(1).to_broadcast([P, NT, E]), ALU.add).then_inc(S["s_lg"], 1)
            dve.wait_ge(S["s_lg"], 1)
            for t in range(NT):
                last = dve.max(v8[:, t, :], lg[:, t, :])
            last.then_inc(S["s_v8"], 1)
            dve.wait_ge(S["s_v8"], 1)
            dve.tensor_tensor(gd[:, :], v8[:, :, 1], v8[:, :, 0], ALU.subtract).then_inc(S["s_gd"], 1)
            for t in range(NT):
                last = dve.max_index(i8[:, t, :], v8[:, t, :], lg[:, t, :])
            last.then_inc(S["s_i8"], 1)
            dve.wait_ge(S["s_i8"], 1)
            dve.tensor_copy(i8f[:, :, :], i8[:, :, :]).then_inc(S["s_g"], 1)
            dve.wait_ge(S["s_ge"], 1)
            dve.tensor_scalar(gd[:, :], ge[:, :], 1.0, None, ALU.add).then_inc(S["s_g"], 1)
            dve.wait_ge(S["s_g"], 2)
            dve.reciprocal(g1[:, :], gd[:, :]).then_inc(S["s_g"], 1)
            for k in range(2):
                dve.tensor_tensor(eq[:, k, :, :], io8[:, :].unsqueeze(1).to_broadcast([P, NT, E]),
                                  i8f[:, :, k:k + 1].to_broadcast([P, NT, E]), ALU.is_equal).then_inc(S["s_g"], 1)
            dve.wait_ge(S["s_g"], 5)
            dve.tensor_tensor(g2[:, :], ge[:, :], g1[:, :], ALU.mult).then_inc(S["s_g"], 1)
            dve.tensor_tensor(eq[:, 0, :, :], eq[:, 0, :, :], g1[:, :].unsqueeze(2).to_broadcast([P, NT, E]), ALU.mult)\
                .then_inc(S["s_g"], 1)
            dve.wait_ge(S["s_g"], 7)
            dve.tensor_tensor(eq[:, 1, :, :], eq[:, 1, :, :], g2[:, :].unsqueeze(2).to_broadcast([P, NT, E]), ALU.mult)\
                .then_inc(S["s_g"], 1)
            dve.wait_ge(S["s_g"], 8)
            dve.tensor_tensor(gate[:, :, :], eq[:, 0, :, :], eq[:, 1, :, :], ALU.add).then_inc(S["s_gate"], 1)
            dve.wait_ge(S["s_a0p"], 1)
            dve.tensor_copy(acc[:, :, :], PS[:, 0:4, :].rearrange("p b (t d) -> p (b t) d", d=D))\
                .then_inc(S["s_a0"], 1)
            dve.wait_ge(S["s_a0"], 1)
            dve.wait_ge(S["s_gate"], 1)
            dve.wait_ge(S["s_ms"], 3)

            with dve.Fori(0, L, 1) as l:
                for h in range(2):
                    if h == 0:
                        dve.wait_ge(S["s_yev"], 12 * l + CR_YEV)
                    ln_stats(4 * l + 2 + h, h, xr, xc)
                    ln_apply(4 * l + 2 + h, h, xr, xc)
                dve.wait_ge(S["c_wA"], 64 * (l + 1))
                for b in range(B):
                    for s in range(2):
                        n = 4 * l + 2 * b + s
                        dve.wait_ge(S["s_qk"], n + 1)
                        dve.tensor_scalar(x32[:, b, s, :], PS[:, 2 * s:2 + 2 * s, :].rearrange("p a n -> p (a n)"),
                                          wA[:, 3 * D + 2 + s:3 * D + 3 + s], QSCALE if s == 0 else 1.0,
                                          ALU.add, ALU.mult).then_inc(S["s_q32"], 1)
                    dve.wait_ge(S["s_v"], 2 * l + b + 1)
                    for a in range(2):
                        last = dve.tensor_tensor(
                            vsb[:, 4 * b:4 * b + 4, 4 * a:4 * a + 4, :].rearrange("p g k e -> p k g e"),
                            PS[:, 4 + 2 * b + a, :].rearrange("p (k g e) -> p k g e", k=4, g=4),
                            wV[:, :].rearrange("p (o g e) -> p o g e", o=1, g=4).to_broadcast([P, 4, 4, G * HD]),
                            ALU.add)
                    last.then_inc(S["s_vev"], 1)
                dve.tensor_copy(gcur[:, :, :], gate[:, :, ds(2 * l, 2)].rearrange("p t e -> p e t")).then_inc(s_gc, 1)
                dve.wait_ge(s_gc, l + 1)
                places = first_places
                for c in range(3):
                    expert_out(l, c)
                for c in range(4, 8):
                    for g in range(3 * (c - 4), 3 * (c - 4) + 3):
                        maxima(8 * l, 0, g)
                    expert_out(l, c - 1)
                neg_max(8 * l, 0)
                expert_out(l, 7)
                places = stage_places

                def stage(u, par):
                    for g in range(len(P1_GROUPS)):
                        maxima(8 * l + u + 1, 1 - par, g)
                    neg_max(8 * l + u + 1, 1 - par)

                with dve.Fori(0, UN // 2 - 1, 1) as i:
                    stage(2 * i, 0)
                    stage(2 * i + 1, 1)
                stage(UN - 2, 0)
                dve.wait_ge(S["c_den"], 32 * l + 32)
                for b in range(B):
                    dve.reciprocal(den[:, b, :], den[:, b, :]).then_inc(S["s_rc"], 1)
                dve.wait_ge(S["c_OT"], 64 * l + 64)
                for b in range(B):
                    dve.tensor_tensor(OT[:, b, :], OT[:, b, :], rT[:, b, :], ALU.mult).then_inc(S["s_onT"], 1)
                dve.wait_ge(S["s_bias"], 2 * l + 1)
                for b in range(B):
                    dve.wait_ge(S["s_wo"], 2 * l + b + 1)
                    dve.tensor_tensor(xr[:, TB * b:TB * b + TB, :],
                                      PS[:, 2 * b:2 * b + 2, :].rearrange("p a (t d) -> p (a t) d", d=D),
                                      xr[:, TB * b:TB * b + TB, :], ALU.add).then_inc(S["s_woev"], 1)
                for h in range(2):
                    dve.wait_ge(S["s_woev"], 2 * l + h + 1)
                    ln_stats(4 * l + 4 + h, h, xr, xc)
                    ln_apply(4 * l + 4 + h, h, xr, xc)
                dve.wait_ge(S["s_bias"], 2 * l + 2)
                for c in range(8, 12):
                    expert_out(l, c)

            dve.wait_ge(S["s_yev"], 12 * L + CR_YEV)
            for h in range(2):
                ln_stats(4 * L + 2 + h, h, xr, xc)
                ln_apply(4 * L + 2 + h, h, xr, xc)
                dve.wait_ge(S["s_lnxc"], 4 * L + 3 + h)
                o = xc[:, TB * h:TB * h + TB, :]
                for k, (other, op) in enumerate(((finw[:, 0:1, :].to_broadcast([P, TB, D]), ALU.mult),
                                                 (finw[:, 1:2, :].to_broadcast([P, TB, D]), ALU.add),
                                                 (xin[:, TB * h:TB * h + TB, :], ALU.add),
                                                 (acc[:, TB * h:TB * h + TB, :], ALU.add))):
                    dve.tensor_tensor(o, o, other, op).then_inc(S["s_fin"], 1)
                    dve.wait_ge(S["s_fin"], 4 * h + k + 1)


def bf16_bits(a):
    import numpy as np
    w = np.ascontiguousarray(a, np.float32).view(np.uint32).astype(np.uint64)
    return ((w + 0x7FFF + ((w >> 16) & 1)) >> 16).astype(np.uint16)


def bf16_parts(a, n=3):
    import numpy as np
    out = []
    r = np.asarray(a, np.float64)
    for _ in range(n):
        bits = bf16_bits(r)
        out.append(bits)
        r = r - (bits.astype(np.uint32) << 16).view(np.float32).astype(np.float64)
    return out


def constants():
    import numpy as np
    one = bf16_bits(1.0)
    big = -1.0e30
    r = np.arange(64)
    m1 = np.zeros((2, 64, 2, P), np.float32)
    m2 = np.zeros((2, 64, 2, P), np.float32)
    for c in range(2):
        pos = 64 * c + r[:, None]
        m1[:, :, c, :] = np.where(pos > np.arange(P)[None, :], big, 0.0)
        m2[:, :, c, :] = np.where(np.arange(P)[None, :] > pos, big, 0.0)
    kcon = np.zeros((H, 16, T), np.uint16)
    qcon = np.zeros((H, 16, T), np.uint16)
    slopes = (2.0 ** (-0.5 * np.arange(1, H + 1))).astype(np.float32)
    for h in range(H):
        pos = slopes[h].astype(np.float64) * np.arange(T)
        for i, part in enumerate(bf16_parts(pos)):
            kcon[h, i] = part
        for i, part in enumerate(bf16_parts(-pos)):
            qcon[h, 3 + i] = part
        qcon[h, 0:3] = one
        kcon[h, 3:6] = one
        kcon[h, 8:11] = one
    return dict(ident=np.eye(P, dtype=np.float32), identb=bf16_bits(np.eye(P)),
                iota=np.tile(np.arange(E, dtype=np.float32), (P, 1)),
                m1=bf16_bits(m1.reshape(P, 2, P)), m2=bf16_bits(m2.reshape(P, 2, P)),
                kcon=kcon.reshape(H, 16, T), qcon=qcon.reshape(H, 16, T))


def kernel(**inputs):
    import numpy as _np
    import concourse.bacc as _bacc
    from concourse import mybir as _mybir
    from concourse.bass_utils import run_bass_kernel_spmd as _run

    a = {k.replace("L0_attn_", "a_").replace("L0_ffn_", "m_"): _np.asarray(v) for k, v in inputs.items()}
    cat = _np.concatenate

    def col(v):
        return v[..., None]

    def tiles(w):
        n = w.shape[0]
        return w.reshape(n, FT, P, D).transpose(0, 2, 1, 3).reshape(n, P, FT * D)

    bi = a["a_in_proj_b"]
    layout = dict(
        x=a["a_x"],
        cA=cat([a["a_in_proj_w"].transpose(0, 2, 1), col(a["a_ln1_w"]), col(a["a_ln1_b"]),
                col(bi[:, 0:D]), col(bi[:, D:2 * D])], axis=2),
        rA=_np.stack([bi[:, 2 * D:], a["a_out_proj_b"], a["a_ffn2_b"]], axis=1),
        cB=cat([a["a_ffn1_w"].transpose(0, 2, 1), tiles(a["a_ffn2_w"].transpose(0, 2, 1)),
                a["a_ffn1_b"].reshape(L, FT, P).transpose(0, 2, 1),
                a["a_out_proj_w"].transpose(0, 2, 1), col(a["a_ln2_w"]), col(a["a_ln2_b"])], axis=2),
        moe=cat([a["m_w1"], tiles(a["m_w2"]), a["m_b1"].reshape(E, FT, P).transpose(0, 2, 1)], axis=2),
        router_w=a["m_router_w"],
        rb_b2=cat([_np.pad(a["m_router_b"], (0, D - E))[None], a["m_b2"]], axis=0),
        fin=_np.stack([a["a_final_w"], a["a_final_b"]]),
    )
    layout.update(constants())
    nc = _bacc.Bacc("TRN2", target_bir_lowering=False, num_devices=1)
    arrays, args = {}, {}
    for name, v in layout.items():
        v = _np.ascontiguousarray(v)
        arrays[f"in_{name}"] = v
        args[name] = nc.dram_tensor(f"in_{name}", v.shape, _mybir.dt.from_np(v.dtype), kind="ExternalInput").ap()
    args["out"] = nc.dram_tensor("out_0", (B, T, D), _mybir.dt.float32, kind="ExternalOutput").ap()
    build(nc, **args)
    r = _run(nc, [arrays], core_ids=[0])
    return r.results[0]["out_0"]
```

```python
from contextlib import ExitStack

import concourse.bass as bass
from concourse import mybir

F32 = mybir.dt.float32
BF16 = mybir.dt.bfloat16
U32 = mybir.dt.uint32
ALU = mybir.AluOpType
ACT = mybir.ActivationFunctionType
AXX = mybir.AxisListType.X
ds = bass.ds

B, T, D, L, H, F, E = 2, 1024, 128, 4, 16, 512, 8
P = 128
HD = D // H
NT = B * T // P
TB = T // P
G = 4
UN = B * H // G
FT = F // P
ROWS = 64
MROW = 56
EPS = 1e-5
QSCALE = float(HD) ** -0.5
Q_PARTS = (0, 0, 1, 0, 2, 1)
K_PARTS = (0, 1, 0, 2, 0, 1)

P1_CHUNKS = [(i, h, c, 512 * c, min(512, P * (i + 1) - 512 * c))
             for i in range(TB) for h in range(G) for c in range(1 + i // 4)]
P1N = len(P1_CHUNKS)
P1L = G * TB // 2
P2_JOBS = [(qh, kt, max(512 * qh, P * kt), 512 * (qh + 1) - max(512 * qh, P * kt))
           for qh in range(2) for kt in range(4 * (qh + 1))]
JOBN = len(P2_JOBS)
SLOTS = 2 * JOBN
TURN_R, TURN_L = 2, 12
H_SLOTS = (4, 6, 8, 10)
Y_SLOTS = (16, 18, 20, 22)
GELU_SLOT = 12
LTURN_OUT = 13
Y0_SLOTS, H1_SLOTS, Y1_SLOTS = (0, 1, 2, 3), (4, 5, 6, 7), (12, 13, 14, 15)
TURN_0 = 16
CH = 6
SCH = 6
DIAG = [kt >= 4 * qh for qh, kt, _, _ in P2_JOBS]


def build(nc, x, cA, rA, cB, moe, router_w, rb_b2, fin, ident, identb, iota, mask, m2, kcon, qcon, out):
    with ExitStack() as ctx:
        def sb(name, shape, dt=F32):
            return ctx.enter_context(nc.sbuf_tensor(name, shape, dt))

        def sem(name):
            return ctx.enter_context(nc.semaphore(name))

        def dram(name, shape, dt=F32):
            return nc.dram_tensor(name, shape, dt, kind="Internal").ap()

        PS = ctx.enter_context(nc.psum_tensor("PS", [P, 8, 512], F32))

        kst = dram("kst", [B, H, ROWS, T], BF16)
        qst = dram("qst", [B, H, ROWS, T], BF16)
        onum = dram("onum", [UN, G * HD, T])
        oden = dram("oden", [UN * G, T])
        orec = dram("orec", [UN * G, T])

        idf = sb("idf", [P, P])
        idb = sb("idb", [P, P], BF16)
        io8 = sb("io8", [P, E])
        mk2 = sb("mk2", [P, P], BF16)
        mkw = sb("mkw", [P, 512])
        mhalf = sb("mhalf", [P, TB])
        rw = sb("rw", [P, E])
        rb = sb("rb", [P, E])
        b2e = sb("b2e", [E, D])
        finw = sb("finw", [P, 2, D])
        wA = sb("wA", [P, 3 * D + 4])
        wV = sb("wV", [P, D])
        wR = sb("wR", [P, 2, D])
        wB = sb("wB", [P, D + 2])
        NW = 2 * F + FT
        wE = [sb(f"wE{i}", [P, NW]) for i in range(3)]
        xin = sb("xin", [P, NT, D])
        xr = sb("xr", [P, NT, D])
        acc = sb("acc", [P, NT, D])
        xc = sb("xc", [P, NT, D])
        xn0T = sb("xn0T", [P, B, T])
        xnT = sb("xnT", [P, B, T])
        st = sb("st", [P, 2, TB, 6])
        mv = sb("mv", [P, 2, TB, 2])
        ve = sb("ve", [P, 2, TB])
        rstd = sb("rstd", [P, 2, TB])
        lg = sb("lg", [P, NT, E])
        v8 = sb("v8", [P, NT, E])
        i8 = sb("i8", [P, NT, E], U32)
        i8f = sb("i8f", [P, NT, E])
        gd = sb("gd", [P, NT])
        ge = sb("ge", [P, NT])
        g1 = sb("g1", [P, NT])
        g2 = sb("g2", [P, NT])
        eq = sb("eq", [P, 2, NT, E])
        gate = sb("gate", [P, NT, E])
        gT = sb("gT", [E, NT * P])
        x32 = sb("x32", [P, B, 2, T])
        OT = x32[:, :, 0, :]
        rT = x32[:, :, 1, :]
        parts = sb("parts", [P, 3, B, 2, T], BF16)
        vsb = sb("vsb", [P, UN, TB, G * HD])
        vbuf = sb("vbuf", [P, 2, TB, G, 32])
        Kop = sb("Kop", [P, 2, 2, T], BF16)
        Qop = sb("Qop", [P, 2, 2, 2, T], BF16)
        mx = sb("mx", [P, 2, TB, G, 2])
        negm = sb("negm", [P, 2, TB, G])
        mres = sb("mres", [P, 2, TB, G])
        mp = sb("mp", [P, 2, TB, G, 3], BF16)
        mrow = sb("mrow", [G * 3, 2, T], BF16)
        PR = sb("PR", [P, 4, 2, 512])
        osb = sb("osb", [P, 2, 512])
        den = sb("den", [P, 2, P])
        hb = sb("hb", [P, 2, FT, 512])
        gcur = sb("gcur", [P, 2, NT])

        names = """c_const c_x c_wA c_wB c_stg0 c_stg1 c_con c_out
            s_lnst s_lnag s_lnve s_lnrs s_lnxc s_lnT s_lnev
            s_ms s_lgp s_lg s_v8 s_i8 s_gd s_ge s_g s_gate s_gTp s_gT s_a0p s_a0
            s_qk s_q32 s_v s_vev s_hi s_r s_mid s_lo s_bias
            s_p1 s_p1m s_negm s_mpool s_turn s_mrow s_vb
            s_s2 s_exp s_pv s_oev s_rc s_onT s_wo s_woev
            s_h s_gelu s_y s_yev s_sh s_shev s_sg s_sy s_syev s_fin""".split()
        S = {n: sem(n) for n in names}
        c_ldl = [sem(f"c_ldl{i}") for i in range(2)]
        c_ldr = [sem(f"c_ldr{i}") for i in range(2)]
        c_m = [[sem(f"c_m{i}{half}") for half in range(2)] for i in range(2)]
        c_o = [sem(f"c_o{i}") for i in range(2)]
        s_gc = sem("s_gc")
        passed = sem("passed")
        c_den = [sem(f"c_den{b}") for b in range(B)]
        c_rec = [sem(f"c_rec{b}") for b in range(B)]
        c_OT = [sem(f"c_OT{b}") for b in range(B)]
        c_stg = [S["c_stg0"], S["c_stg1"]]
        ODMA = 16 * 5
        CR_EXP, CR_PV, CR_OEV, CR_GELU, CR_Y, CR_YEV, CR_M, CR_SG, CR_SY = 2, 2, 1, 4, 2, 4, 1, 1, 1

        block = ctx.enter_context(nc.Block())
        kcov = kcon.bitcast(BF16).rearrange("h r t -> h (r t)")
        qcov = qcon.bitcast(BF16).rearrange("h r t -> h (r t)")
        xv = x.rearrange("b (t p) d -> p (b t) d", p=P)
        ov = out.rearrange("b (t p) d -> p (b t) d", p=P)
        kun = kst.rearrange("b (g a j) r t -> (b g) (j r) a t", a=2, j=2)
        qun = qst.rearrange("b (g a j) r t -> (b g) (j r) a t", a=2, j=2)

        TURN = PS[:, 7, :].bitcast(BF16)[0:3 * G, :]
        x0 = xn0T[:, :, :].rearrange("p b t -> p (b t)")

        def wait_apart(eng, semaphore, value):
            eng.wait_ge(semaphore, value)
            eng.sem_inc(passed, 1)

        @block.sync
        def _(sp):
            for h in range(2):
                sp.dma_start(xin[:, TB * h:TB * h + TB, :], xv[:, TB * h:TB * h + TB, :]).then_inc(S["c_x"], 16)
            for dst, src in ((idf[:, :], ident), (idb[:, :], identb.bitcast(BF16)), (io8[:, :], iota), (mkw[:, :], mask),
                             (mk2[:, :], m2.bitcast(BF16)),
                             (rw[:, :], router_w),
                             (rb[:, :], rb_b2[0:1, 0:E].to_broadcast([P, E])),
                             (b2e[:, :], rb_b2[1:1 + E, :]),
                             (finw[:, :, :], fin.unsqueeze(0).to_broadcast([P, 2, D]))):
                sp.dma_start(dst, src).then_inc(S["c_const"], 16)
            for b in range(B):
                for dst, src in ((kst, kcov), (qst, qcov)):
                    sp.dma_start(dst[b, :, 6 * HD:ROWS, :].rearrange("h r t -> h (r t)"), src)\
                        .then_inc(S["c_con"], 16)
            sp.wait_ge(S["c_con"], 64)
            sp.wait_ge(S["s_ms"], 4)

            def load(u, U, par, half):
                c = (c_ldl, c_ldr)[half][par]
                cols = slice(512 * half, 512 * half + 512)
                for j in range(2):
                    r = slice(ROWS * j, ROWS * j + ROWS)
                    sp.dma_start(Qop[r, par, j, :, cols], qun[ds(u, 1), r, :, cols].rearrange("u p a t -> (u p) a t"))\
                        .then_inc(c, 16)
                sp.dma_start(Kop[:, par, :, cols], kun[ds(u, 1), :, :, cols].rearrange("u p a t -> (u p) a t"))\
                    .then_inc(c, 16)

            def minus_max(U, par, half):
                sp.wait_ge(S["s_mrow"], 2 * U + half + 1 + CR_M)
                cols = slice(512 * half, 512 * half + 512)
                for h in range(G):
                    sp.dma_start(Qop[64 * (h % 2) + MROW:64 * (h % 2) + MROW + 3, par, h % 2, h // 2, cols],
                                 mrow[3 * h:3 * h + 3, par, cols]).then_inc(c_m[par][half], 16)

            def outputs(u, U, qh):
                sp.wait_ge(S["s_oev"], 2 * U + qh + 1 + CR_OEV)
                cols = slice(512 * qh, 512 * qh + 512)
                for h in range(G):
                    sp.dma_start(onum[ds(u, 1), HD * h:HD * h + HD, cols].rearrange("u r t -> (u r) t"),
                                 osb[32 * h:32 * h + HD, qh, :]).then_inc(c_o[qh], 16)
                sp.dma_start(oden[ds(G * u, G), cols], osb[HD:P:32, qh, :]).then_inc(c_o[qh], 16)

            def stage(l, u, par, more=True, loads=True):
                U = 8 * l + u
                minus_max(U, par, 1)
                outputs(u, U, 0)
                if more:
                    minus_max(U + 1, 1 - par, 0)
                if loads:
                    sp.wait_ge(S["s_s2"], 24 * U + 16)
                    load(u + 2, U, par, 0)
                    sp.wait_ge(S["s_s2"], 24 * U + 24)
                    load(u + 2, U, par, 1)
                outputs(u, U, 1)

            def normaliser(l, b):
                rows = slice(UN * G // 2 * b, UN * G // 2 * (b + 1))
                for qh in range(2):
                    sp.wait_ge(c_o[qh], ODMA * (8 * l + 4 * b + 4) + ODMA)
                sp.dma_start(den[:, b, :], oden[rows, :].rearrange("h (c n) -> (h c) n", n=P)).then_inc(c_den[b], 16)
                sp.dma_start(OT[:, b, :], onum[4 * b:4 * b + 4, :, :].rearrange("u r t -> (u r) t"))\
                    .then_inc(c_OT[b], 16)
                sp.wait_ge(S["s_rc"], 2 * l + b + 1)
                sp.dma_start(orec[rows, :].rearrange("h (c n) -> (h c) n", n=P), den[:, b, :])\
                    .then_inc(c_rec[b], 16)
                sp.wait_ge(c_rec[b], 16 * l + 16)
                sp.dma_start(rT[:, b, :], orec[rows, :].unsqueeze(1).to_broadcast([H, HD, T])).then_inc(c_OT[b], 16)

            with sp.Fori(0, L, 1) as l:
                sp.dma_start(wA[:, :], cA[ds(l, 1), :, :].rearrange("l p n -> (l p) n")).then_inc(S["c_wA"], 16)
                sp.dma_start(wV[:, :], rA[ds(l, 1), 0, :].to_broadcast([P, D])).then_inc(S["c_wA"], 16)
                for e in range(2):
                    sp.dma_start(wE[e][:, :], moe[ds(2 * l + e, 1), :, :].rearrange("l p n -> (l p) n"))\
                        .then_inc(S["c_wA"], 16)
                for b in range(B):
                    for s, stg, which in ((0, qst, Q_PARTS), (1, kst, K_PARTS)):
                        for part, done in ((0, "s_hi"), (1, "s_mid"), (2, "s_lo")):
                            sp.wait_ge(S[done], 4 * l + 2 * b + s + 1)
                            for blk in range(6):
                                if which[blk] == part:
                                    sp.dma_start(stg[b, :, HD * blk:HD * blk + HD, :], parts[:, part, b, s, :])\
                                        .then_inc(c_stg[b], 16)
                    wait_apart(sp, c_stg[b], 192 * (l + 1))
                    if b == 0:
                        for u in range(2):
                            for half in range(2):
                                load(u, 8 * l + u, u, half)
                        sp.dma_start(wB[:, :], cB[ds(l, 1), :, NW:]
                                     .rearrange("l p n -> (l p) n")).then_inc(S["c_wB"], 16)
                        sp.dma_start(wE[2][:, :], cB[ds(l, 1), :, 0:NW]
                                     .rearrange("l p n -> (l p) n")).then_inc(S["c_wB"], 16)
                        sp.dma_start(wR[:, :, :], rA[ds(l, 1), 1:3, :].to_broadcast([P, 2, D]))\
                            .then_inc(S["c_wB"], 16)
                minus_max(8 * l, 0, 0)
                with sp.Fori(0, UN // 2 - 1, 1) as i:
                    stage(l, 2 * i, 0)
                    stage(l, 2 * i + 1, 1)
                minus_max(8 * l + UN - 2, 0, 1)
                normaliser(l, 0)
                outputs(UN - 2, 8 * l + UN - 2, 0)
                minus_max(8 * l + UN - 1, 1, 0)
                outputs(UN - 2, 8 * l + UN - 2, 1)
                stage(l, UN - 1, 1, more=False, loads=False)
                normaliser(l, 1)
            for h in range(2):
                sp.wait_ge(S["s_fin"], 4 * h + 4)
                sp.dma_start(ov[:, TB * h:TB * h + TB, :], xc[:, TB * h:TB * h + TB, :]).then_inc(S["c_out"], 16)
            sp.wait_ge(S["c_out"], 32)

        @block.gpsimd
        def _(pool):
            pool.memset(mhalf[:, :], -0.5).then_inc(S["s_ms"], 1)
            pool.memset(vbuf[:, :, :, :, :], 1.0).then_inc(S["s_ms"], 1)
            pool.memset(mx[:, :, :, :, :], -3.0e38).then_inc(S["s_ms"], 1)
            pool.memset(Qop[:, :, :, :, :], 0.0).then_inc(S["s_ms"], 1)
            pool.wait_ge(S["s_ms"], 4)

            def rstd_of(idx, h):
                pool.wait_ge(S["s_lnve"], idx + 1)
                pool.tensor_tensor(rstd[:, h, :], ve[:, h, :], mhalf[:, :], ALU.pow).then_inc(S["s_lnrs"], 1)

            def split(l, b, s):
                n = 4 * l + 2 * b + s
                pool.wait_ge(S["s_hi"], n + 1)
                pool.tensor_tensor(x32[:, b, s, :], x32[:, b, s, :], parts[:, 0, b, s, :], ALU.subtract)\
                    .then_inc(S["s_r"], 1)
                pool.wait_ge(S["s_mid"], n + 1)
                pool.tensor_tensor(parts[:, 2, b, s, :], x32[:, b, s, :], parts[:, 1, b, s, :], ALU.subtract)\
                    .then_inc(S["s_lo"], 1)

            def add_bias(row, h):
                half = xr[:, TB * h:TB * h + TB, :]
                pool.tensor_tensor(half, half, wR[:, row:row + 1, :].to_broadcast([P, TB, D]), ALU.add)\
                    .then_inc(S["s_bias"], 1)

            def values(u, par):
                pool.tensor_copy(vbuf[:, par, :, :, 0:HD],
                                 vsb[:, ds(u, 1), :, :].rearrange("p u k (g e) -> p (u k) g e", g=G))\
                    .then_inc(S["s_vb"], 1)

            def max_parts(U, par, half):
                n = 2 * U + half
                tiles = slice(4 * half, 4 * half + 4)
                wait_apart(pool, S["s_negm"], n + 1)
                pool.tensor_copy(mp[:, par, tiles, :, 0], negm[:, par, tiles, :]).then_inc(S["s_mpool"], 1)
                pool.wait_ge(S["s_mpool"], 4 * n + 1)
                pool.tensor_tensor(mres[:, par, tiles, :], negm[:, par, tiles, :], mp[:, par, tiles, :, 0],
                                   ALU.subtract).then_inc(S["s_mpool"], 1)
                wait_apart(pool, S["s_mpool"], 4 * n + 2)
                pool.tensor_copy(mp[:, par, tiles, :, 1], mres[:, par, tiles, :]).then_inc(S["s_mpool"], 1)
                pool.wait_ge(S["s_mpool"], 4 * n + 3)
                pool.tensor_tensor(mp[:, par, tiles, :, 2], mres[:, par, tiles, :], mp[:, par, tiles, :, 1],
                                   ALU.subtract).then_inc(S["s_mpool"], 1)

            def stage(l, u, par):
                U = 8 * l + u
                max_parts(U, par, 1)
                wait_apart(pool, S["s_pv"], 12 * U + CR_PV)
                values(u + 1, 1 - par)
                max_parts(U + 1, 1 - par, 0)

            for h in range(2):
                rstd_of(h, h)
            with pool.Fori(0, L, 1) as l:
                for h in range(2):
                    rstd_of(4 * l + 2 + h, h)
                for b in range(B):
                    for s in range(2):
                        split(l, b, s)
                wait_apart(pool, S["s_vev"], 2 * l + 2)
                values(0, 0)
                max_parts(8 * l, 0, 0)
                pool.wait_ge(S["c_wB"], 48 * (l + 1))
                pool.wait_ge(S["s_lnxc"], 4 * l + 4)
                for h in range(2):
                    add_bias(0, h)
                with pool.Fori(0, UN // 2 - 1, 1) as i:
                    stage(l, 2 * i, 0)
                    stage(l, 2 * i + 1, 1)
                stage(l, UN - 2, 0)
                max_parts(8 * l + UN - 1, 1, 1)
                for h in range(2):
                    rstd_of(4 * l + 4 + h, h)
                    pool.wait_ge(S["s_lnxc"], 4 * l + 5 + h)
                    add_bias(1, h)
            for h in range(2):
                rstd_of(4 * L + 2 + h, h)

        @block.scalar
        def _(act):
            act.sem_inc(S["s_exp"], CR_EXP)
            act.sem_inc(S["s_oev"], CR_OEV)
            act.sem_inc(S["s_gelu"], CR_GELU)
            act.sem_inc(S["s_mrow"], CR_M)
            act.sem_inc(S["s_sg"], CR_SG)

            def ln_out(idx, h, bank, dst, w):
                act.wait_ge(S["s_lnT"], idx + 1)
                src = PS[:, bank:bank + 2, :]
                if w is None:
                    act.activation(dst[:, h, :], src, ACT.Copy).then_inc(S["s_lnev"], 1)
                else:
                    act.activation(dst[:, h, :], src, ACT.Identity, scale=w[0], bias=w[1]).then_inc(S["s_lnev"], 1)

            def gelu(l, c):
                m = CH * l + c
                for f in range(FT):
                    act.wait_ge(S["s_h"], 4 * m + f + 1)
                    if f == 0:
                        act.wait_ge(S["s_y"], m - 1 + CR_Y)
                    act.activation(hb[:, c % 2, f, :], PS[:, f, :], ACT.Gelu,
                                   bias=wE[min(c, 2)][:, 2 * F + f:2 * F + f + 1]).then_inc(S["s_gelu"], 1)

            def turn_out(U, par, half):
                act.wait_ge(S["s_turn"], 2 * U + half + 1)
                act.activation(mrow[:, par, 512 * half:512 * half + 512], TURN[:, 512 * half:512 * half + 512],
                               ACT.Copy).then_inc(S["s_mrow"], 1)

            def exps(U, c):
                t, a = c // 2, c % 2
                n = P2_JOBS[t][3]
                act.wait_ge(S["s_s2"], 24 * U + c + 1)
                if a == 0:
                    act.wait_ge(S["s_pv"], 12 * U + t - 1 + CR_PV)
                act.activation(PR[:, c % 4, :, 0:n], PS[:, 2 * (c % 2):2 * (c % 2) + 2, 0:n], ACT.Exp)\
                    .then_inc(S["s_exp"], 1)

            def sums_out(U, qh):
                act.wait_ge(S["s_pv"], 12 * U + (4, 12)[qh] + CR_PV)
                act.wait_ge(c_o[qh], ODMA * U + ODMA)
                act.activation(osb[:, qh, :], PS[:, 4, :], ACT.Copy).then_inc(S["s_oev"], 1)

            def stage(l, u, par, i=None, more=True):
                U = 8 * l + u
                for c in range(SLOTS):
                    exps(U, c)
                    if c == TURN_R:
                        turn_out(U, par, 1)
                    if c == 9:
                        sums_out(U, 0)
                    if c == GELU_SLOT and i is not None:
                        m = SCH * l + u
                        act.wait_ge(S["s_shev"], 4 * m + 4)
                        act.wait_ge(S["s_sy"], m + CR_SY)
                        act.activation(hb[:, 1, :, :], hb[:, 0, :, :], ACT.Gelu).then_inc(S["s_sg"], 1)
                    if c == LTURN_OUT and more:
                        turn_out(U + 1, 1 - par, 0)
                sums_out(U, 1)

            for h in range(2):
                ln_out(h, h, 4 + 2 * h, xn0T, None)
            act.wait_ge(S["s_gd"], 1)
            act.activation(ge[:, :], gd[:, :], ACT.Exp).then_inc(S["s_ge"], 1)
            act.wait_ge(S["s_gTp"], 1)
            act.activation(gT[:, :], PS[0:E, 4:8, :], ACT.Copy).then_inc(S["s_gT"], 1)
            with act.Fori(0, L, 1) as l:
                act.wait_ge(S["c_wA"], 64 * (l + 1))
                for h in range(2):
                    ln_out(4 * l + 2 + h, h, 4 + 2 * h, xnT, (wA[:, 3 * D:3 * D + 1], wA[:, 3 * D + 1:3 * D + 2]))
                for b in range(B):
                    for s in range(2):
                        n = 4 * l + 2 * b + s
                        act.wait_ge(S["s_q32"], n + 1)
                        act.activation(parts[:, 0, b, s, :], x32[:, b, s, :], ACT.Copy).then_inc(S["s_hi"], 1)
                        act.wait_ge(S["s_r"], n + 1)
                        act.activation(parts[:, 1, b, s, :], x32[:, b, s, :], ACT.Copy).then_inc(S["s_mid"], 1)
                for c in range(2):
                    gelu(l, c)
                turn_out(8 * l, 0, 0)
                with act.Fori(0, UN // 2 - 1, 1) as i:
                    stage(l, 2 * i, 0, i)
                    stage(l, 2 * i + 1, 1, i)
                stage(l, UN - 2, 0)
                stage(l, UN - 1, 1, more=False)
                act.wait_ge(S["c_wB"], 48 * (l + 1))
                for h in range(2):
                    ln_out(4 * l + 4 + h, h, 5, xnT, (wB[:, D:D + 1], wB[:, D + 1:D + 2]))
                    for c in range(2 + 2 * h, 4 + 2 * h):
                        gelu(l, c)


        @block.tensor
        def _(pe):
            pe.sem_inc(S["s_pv"], CR_PV)
            pe.sem_inc(S["s_y"], CR_Y)
            pe.sem_inc(S["s_sy"], CR_SY)

            def ln_turn(idx, h, bank, src):
                pe.wait_ge(S["s_lnxc"], idx + 1)
                for t in range(TB):
                    last = pe.transpose(PS[:, bank + t // 4, P * (t % 4):P * (t % 4) + P], src[:, TB * h + t, :],
                                        idf[:, :])
                last.then_inc(S["s_lnT"], 1)

            def h_piece(l, c, src, f):
                m = CH * l + c
                n = 3 if c < 2 else c - 2
                pe.wait_ge(S["s_gelu"], 4 * m - 4 + f + 1 + CR_GELU)
                pe.matmul(PS[:, f, :], wE[min(c, 2)][:, P * f:P * f + P],
                          src[:, n // 2, 512 * (n % 2):512 * (n % 2) + 512], start=True, stop=True)\
                    .then_inc(S["s_h"], 1)

            def y_piece(l, c, j):
                m = CH * l + c
                w = wE[min(c, 2)]
                if j == 0:
                    pe.wait_ge(S["s_gelu"], 4 * m + 4 + CR_GELU)
                    pe.wait_ge(S["s_yev"], m + CR_YEV)
                for f in range(FT):
                    last = pe.matmul(PS[:, 4, P * j:P * j + P], hb[:, c % 2, f, P * j:P * j + P],
                                     w[:, F + P * f:F + P * f + P], start=(f == 0), stop=(f == FT - 1))
                if j == 3:
                    last.then_inc(S["s_y"], 1)

            def p1_chunk(U, par, nth, k, first=False):
                i, h, c, k0, n = P1_CHUNKS[k]
                if k == 0:
                    operands(nth, par, 0)
                if k == P1L:
                    operands(nth, par, 1)
                if k >= 2 or not first:
                    pe.wait_ge(S["s_p1m"], P1N * U + k - 1)
                pe.matmul(PS[:, 5 + k % 2, 0:n], Qop[:, par, h % 2, h // 2, P * i:P * i + P],
                          Kop[:, par, h // 2, k0:k0 + n], start=True, stop=True).then_inc(S["s_p1"], 1)

            def operands(n, par, half):
                pe.wait_ge((c_ldl, c_ldr)[half][par], 48 * (n + 1))

            def turn(U, par, half):
                pe.wait_ge(S["s_mpool"], 4 * (2 * U + half) + 4)
                for i in range(4 * half, 4 * half + 4):
                    last = pe.transpose(TURN[:, P * i:P * i + P],
                                        mp[:, par, i, :, :].rearrange("p g c -> p (g c)"), idb[:, :])
                last.then_inc(S["s_turn"], 1)

            def stage_h(U, m, par, i, f):
                if f == 0:
                    pe.wait_ge(S["s_mrow"], 2 * U + 2 + CR_M)
                else:
                    pe.wait_ge(S["s_shev"], 4 * m + f)
                pe.matmul(PS[:, 7, :], wE[par][:, P * f:P * f + P], x0[:, ds(512 * i, 512)],
                          start=True, stop=True).then_inc(S["s_sh"], 1)

            def stage_y(U, m, par, j):
                if j == 0:
                    pe.wait_ge(S["s_sg"], m + 1 + CR_SG)
                    pe.wait_ge(S["s_mrow"], 2 * U + 3 + CR_M)
                for f in range(FT):
                    last = pe.matmul(PS[:, 7, P * j:P * j + P], hb[:, 1, f, P * j:P * j + P],
                                     wE[par][:, F + P * f:F + P * f + P], start=(f == 0), stop=(f == FT - 1))
                if j == 3:
                    last.then_inc(S["s_sy"], 1)

            def p2_pair(U, par, nth, c):
                t, a = c // 2, c % 2
                qh, kt, q0, n = P2_JOBS[t]
                if c == 0 or c == 8:
                    pe.wait_ge(c_m[par][c // 8], 64 * (nth + 1))
                pe.wait_ge(S["s_exp"], 24 * U + c - 1 + CR_EXP)
                for j in range(2):
                    bank = PS[:, 2 * (c % 2) + j, :]
                    last = pe.matmul(bank[:, 0:n], Kop[:, par, a, P * kt:P * kt + P], Qop[:, par, j, a, q0:q0 + n],
                                     start=True, stop=not DIAG[t])
                    if DIAG[t]:
                        last = pe.matmul(bank[:, 0:P], mk2[:, :], idb[:, :], start=False, stop=True)
                last.then_inc(S["s_s2"], 1)

            def p2_values(U, par, t):
                qh, kt, q0, n = P2_JOBS[t]
                if t == 0:
                    pe.wait_ge(S["s_vb"], U + 1)
                if kt == 0:
                    pe.wait_ge(S["s_oev"], 2 * U + qh + CR_OEV)
                pe.wait_ge(S["s_exp"], 24 * U + 2 * t + 2 + CR_EXP)
                for h in range(G):
                    last = pe.matmul(PS[32 * h:32 * h + 32, 4, q0 - 512 * qh:512], vbuf[:, par, kt, h, :],
                                     PR[:, 2 * (t % 2) + h // 2, h % 2, 0:n],
                                     start=(kt == 0), stop=(kt == 4 * qh + 3))
                last.then_inc(S["s_pv"], 1)

            def stage(l, u, par, nth, i=None, more=True):
                U = 8 * l + u
                m = SCH * l + u
                for s in range(SLOTS):
                    if more:
                        p1_chunk(U + 1, 1 - par, nth + par, 2 * s)
                    p2_pair(U, par, nth, s)
                    if more:
                        p1_chunk(U + 1, 1 - par, nth + par, 2 * s + 1)
                    if s == TURN_R:
                        pe.wait_ge(S["s_mrow"], 2 * U + 1 + CR_M)
                        if i is not None:
                            pe.wait_ge(S["s_syev"], m + CR_SY)
                        elif more:
                            pe.wait_ge(S["s_syev"], SCH * l + SCH + CR_SY)
                        turn(U, par, 1)
                    if s == TURN_L and more:
                        if i is not None:
                            pe.wait_ge(S["s_shev"], 4 * m + 4)
                        else:
                            pe.wait_ge(S["s_mrow"], 2 * U + 2 + CR_M)
                        turn(U + 1, 1 - par, 0)
                    if i is not None and s in H_SLOTS:
                        stage_h(U, m, par, i, H_SLOTS.index(s))
                    if i is not None and s in Y_SLOTS:
                        stage_y(U, m, par, Y_SLOTS.index(s))
                    if s % 2 == 1 and s >= 3:
                        p2_values(U, par, s // 2 - 1)
                    if not more and s == 12:
                        attention_out(l, 0)
                p2_values(U, par, JOBN - 1)

            def attention_out(l, b):
                pe.wait_ge(S["c_wB"], 48 * (l + 1))
                pe.wait_ge(S["s_onT"], 2 * l + b + 1)
                for t in range(TB):
                    last = pe.matmul(PS[:, 5 + t // 4, P * (t % 4):P * (t % 4) + P],
                                     OT[:, b, P * t:P * t + P], wB[:, 0:D], start=True, stop=True)
                last.then_inc(S["s_wo"], 1)

            pe.wait_ge(S["c_const"], 16 * 9)
            for h in range(2):
                ln_turn(h, h, 4 + 2 * h, xr)
            pe.wait_ge(S["s_lnev"], 2)
            for t in range(NT):
                last = pe.matmul(PS[:, 4, E * t:E * t + E], xn0T[:, t // TB, P * (t % TB):P * (t % TB) + P], rw[:, :],
                                 start=True, stop=True)
            last.then_inc(S["s_lgp"], 1)
            pe.wait_ge(S["s_gate"], 1)
            for t in range(NT):
                last = pe.transpose(PS[0:E, 4 + t // 4, P * (t % 4):P * (t % 4) + P], gate[:, t, :], idf[:, :])
            last.then_inc(S["s_gTp"], 1)
            pe.wait_ge(S["s_gT"], 1)
            for t in range(NT):
                last = pe.matmul(PS[:, t // 4, P * (t % 4):P * (t % 4) + P], gT[:, P * t:P * t + P], b2e[:, :],
                                 start=True, stop=True)
            last.then_inc(S["s_a0p"], 1)
            pe.wait_ge(S["s_a0"], 1)

            with pe.Fori(0, L, 1) as l:
                for h in range(2):
                    ln_turn(4 * l + 2 + h, h, 4 + 2 * h, xc)
                pe.wait_ge(S["c_wA"], 64 * (l + 1))
                for b in range(B):
                    pe.wait_ge(S["s_lnev"], 4 * l + 3 + b)
                    for s in range(2):
                        if b == 1:
                            pe.wait_ge(S["s_q32"], 4 * l + s + 1)
                        for n in range(2):
                            last = pe.matmul(PS[:, 2 * s + n, :], wA[:, D * s:D * s + D],
                                             xnT[:, b, 512 * n:512 * n + 512], start=True, stop=True)
                        last.then_inc(S["s_qk"], 1)
                    for t in range(TB):
                        last = pe.matmul(PS[:, 4 + 2 * b + t // 4, P * (t % 4):P * (t % 4) + P],
                                         xnT[:, b, P * t:P * t + P], wA[:, 2 * D:3 * D], start=True, stop=True)
                    last.then_inc(S["s_v"], 1)
                pe.wait_ge(S["s_vev"], 2 * l + 2)
                pe.wait_ge(S["s_q32"], 4 * l + 4)
                for f in range(FT):
                    h_piece(l, 0, xn0T, f)
                for s in range(SLOTS):
                    for k in (2 * s, 2 * s + 1):
                        p1_chunk(8 * l, 0, 4 * l, k, first=True)
                    if s in Y0_SLOTS:
                        y_piece(l, 0, Y0_SLOTS.index(s))
                    if s in H1_SLOTS:
                        h_piece(l, 1, xn0T, H1_SLOTS.index(s))
                    if s in Y1_SLOTS:
                        y_piece(l, 1, Y1_SLOTS.index(s))
                    if s == TURN_0:
                        turn(8 * l, 0, 0)
                wait_apart(pe, S["s_yev"], CH * l + 2 + CR_YEV)
                with pe.Fori(0, UN // 2 - 1, 1) as i:
                    stage(l, 2 * i, 0, 4 * l + i, i)
                    stage(l, 2 * i + 1, 1, 4 * l + i, i)
                stage(l, UN - 2, 0, 4 * l + 3)
                stage(l, UN - 1, 1, 4 * l + 3, more=False)
                pe.wait_ge(S["s_oev"], 16 * l + 16 + CR_OEV)
                for h in range(2):
                    if h == 1:
                        attention_out(l, 1)
                    ln_turn(4 * l + 4 + h, h, 5, xc)
                    pe.wait_ge(S["s_lnev"], 4 * l + 5 + h)
                    for c in (2 + 2 * h, 3 + 2 * h):
                        for f in range(FT):
                            h_piece(l, c, xnT, f)
                    for c in (2 + 2 * h, 3 + 2 * h):
                        for j in range(4):
                            y_piece(l, c, j)

        @block.vector
        def _(dve):
            dve.sem_inc(S["s_yev"], CR_YEV)
            dve.sem_inc(S["s_syev"], CR_SY)
            for qh in range(2):
                dve.sem_inc(c_o[qh], ODMA)

            def ln_stats(idx, h, src, dst):
                for t in range(TB):
                    last = dve.bn_stats(st[:, h, t, :], src[:, TB * h + t, :])
                last.then_inc(S["s_lnst"], 1)
                wait_apart(dve, S["s_lnst"], idx + 1)
                for t in range(TB):
                    last = dve.bn_aggr(mv[:, h, t, :], st[:, h, t, :])
                last.then_inc(S["s_lnag"], 1)
                dve.wait_ge(S["s_lnag"], idx + 1)
                dve.tensor_scalar(ve[:, h, :], mv[:, h, :, 1], EPS, None, ALU.add).then_inc(S["s_lnve"], 1)

            def ln_apply(idx, h, src, dst):
                dve.wait_ge(S["s_lnrs"], idx + 1)
                for t in range(TB):
                    last = dve.tensor_scalar(dst[:, TB * h + t, :], src[:, TB * h + t, :], mv[:, h, t, 0:1],
                                             rstd[:, h, t:t + 1], ALU.subtract, ALU.mult)
                last.then_inc(S["s_lnxc"], 1)

            def expert_out(l, c):
                m = CH * l + c
                dve.wait_ge(S["s_y"], m + 1 + CR_Y)
                if c < 2:
                    dve.wait_ge(S["s_yev"], m + CR_YEV)
                    for j in range(4):
                        t = 12 + j
                        last = dve.scalar_tensor_tensor(out=acc[:, t, :], in0=PS[:, 4, P * j:P * j + P],
                                                        scalar=gcur[:, c, t:t + 1], in1=acc[:, t, :],
                                                        op0=ALU.mult, op1=ALU.add)
                else:
                    t = 4 * (c - 2)
                    last = dve.tensor_tensor(xr[:, t:t + 4, :], PS[:, 4, :].rearrange("p (t d) -> p t d", t=4),
                                             xr[:, t:t + 4, :], ALU.add)
                last.then_inc(S["s_yev"], 1)

            def stage_h_out(m, par, f):
                dve.wait_ge(S["s_sh"], 4 * m + f + 1)
                if f == 0:
                    dve.wait_ge(S["s_sg"], m + CR_SG)
                dve.tensor_scalar(hb[:, 0, f, :], PS[:, 7, :], wE[par][:, 2 * F + f:2 * F + f + 1], None, ALU.add)\
                    .then_inc(S["s_shev"], 1)

            def stage_y_out(m, par, i):
                dve.wait_ge(S["s_sy"], m + 1 + CR_SY)
                dve.wait_ge(S["s_syev"], m + CR_SY)
                for j in range(4):
                    a = acc[:, ds(4 * i + j, 1), :].rearrange("p t d -> p (t d)")
                    last = dve.scalar_tensor_tensor(out=a, in0=PS[:, 7, P * j:P * j + P],
                                                    scalar=gcur[:, par, ds(4 * i + j, 1)], in1=a,
                                                    op0=ALU.mult, op1=ALU.add)
                last.then_inc(S["s_syev"], 1)

            def maximum(U, par, k):
                i, h, c, k0, n = P1_CHUNKS[k]
                chunk = PS[:, 5 + k % 2, 0:n]
                if k0 + n == P * (i + 1):
                    wait_apart(dve, S["s_p1"], P1N * U + k + 1)
                    dve.tensor_tensor_reduce(chunk, chunk, mkw[:, 512 - n:512], 1.0, -3.0e38, ALU.add, ALU.max,
                                             mx[:, par, i, h, c:c + 1]).then_inc(S["s_p1m"], 1)
                else:
                    dve.wait_ge(S["s_p1"], P1N * U + k + 1)
                    dve.tensor_reduce(mx[:, par, i, h, c:c + 1], chunk, AXX, ALU.max).then_inc(S["s_p1m"], 1)
                if k == P1L - 1 or k == P1N - 1:
                    tiles = slice(0, 4) if k == P1L - 1 else slice(4, 8)
                    dve.wait_ge(S["s_p1m"], P1N * U + k + 1)
                    dve.tensor_reduce(negm[:, par, tiles, :], mx[:, par, tiles, :, :], AXX, ALU.max, negate=True)\
                        .then_inc(S["s_negm"], 1)

            for h in range(2):
                dve.wait_ge(S["c_x"], 16 * 2)
                ln_stats(h, h, xin, xr)
                ln_apply(h, h, xin, xr)
            dve.wait_ge(S["c_const"], 16 * 9)
            dve.wait_ge(S["s_lgp"], 1)
            dve.tensor_tensor(lg[:, :, :], PS[:, 4, 0:NT * E].rearrange("p (t e) -> p t e", e=E),
                              rb[:, :].unsqueeze(1).to_broadcast([P, NT, E]), ALU.add).then_inc(S["s_lg"], 1)
            dve.wait_ge(S["s_lg"], 1)
            for t in range(NT):
                last = dve.max(v8[:, t, :], lg[:, t, :])
            last.then_inc(S["s_v8"], 1)
            dve.wait_ge(S["s_v8"], 1)
            dve.tensor_tensor(gd[:, :], v8[:, :, 1], v8[:, :, 0], ALU.subtract).then_inc(S["s_gd"], 1)
            for t in range(NT):
                last = dve.max_index(i8[:, t, :], v8[:, t, :], lg[:, t, :])
            last.then_inc(S["s_i8"], 1)
            dve.wait_ge(S["s_i8"], 1)
            dve.tensor_copy(i8f[:, :, :], i8[:, :, :]).then_inc(S["s_g"], 1)
            dve.wait_ge(S["s_ge"], 1)
            dve.tensor_scalar(gd[:, :], ge[:, :], 1.0, None, ALU.add).then_inc(S["s_g"], 1)
            dve.wait_ge(S["s_g"], 2)
            dve.reciprocal(g1[:, :], gd[:, :]).then_inc(S["s_g"], 1)
            for k in range(2):
                dve.tensor_tensor(eq[:, k, :, :], io8[:, :].unsqueeze(1).to_broadcast([P, NT, E]),
                                  i8f[:, :, k:k + 1].to_broadcast([P, NT, E]), ALU.is_equal).then_inc(S["s_g"], 1)
            dve.wait_ge(S["s_g"], 5)
            dve.tensor_tensor(g2[:, :], ge[:, :], g1[:, :], ALU.mult).then_inc(S["s_g"], 1)
            dve.tensor_tensor(eq[:, 0, :, :], eq[:, 0, :, :], g1[:, :].unsqueeze(2).to_broadcast([P, NT, E]), ALU.mult)\
                .then_inc(S["s_g"], 1)
            dve.wait_ge(S["s_g"], 7)
            dve.tensor_tensor(eq[:, 1, :, :], eq[:, 1, :, :], g2[:, :].unsqueeze(2).to_broadcast([P, NT, E]), ALU.mult)\
                .then_inc(S["s_g"], 1)
            dve.wait_ge(S["s_g"], 8)
            dve.tensor_tensor(gate[:, :, :], eq[:, 0, :, :], eq[:, 1, :, :], ALU.add).then_inc(S["s_gate"], 1)
            dve.wait_ge(S["s_a0p"], 1)
            dve.tensor_copy(acc[:, :, :], PS[:, 0:4, :].rearrange("p b (t d) -> p (b t) d", d=D))\
                .then_inc(S["s_a0"], 1)
            dve.wait_ge(S["s_a0"], 1)
            dve.wait_ge(S["s_gate"], 1)
            dve.wait_ge(S["s_ms"], 4)

            with dve.Fori(0, L, 1) as l:
                for h in range(2):
                    if h == 0:
                        dve.wait_ge(S["s_yev"], CH * l + CR_YEV)
                    ln_stats(4 * l + 2 + h, h, xr, xc)
                    ln_apply(4 * l + 2 + h, h, xr, xc)
                dve.wait_ge(S["c_wA"], 64 * (l + 1))
                for b in range(B):
                    for s in range(2):
                        n = 4 * l + 2 * b + s
                        dve.wait_ge(S["s_qk"], n + 1)
                        dve.tensor_scalar(x32[:, b, s, :], PS[:, 2 * s:2 + 2 * s, :].rearrange("p a n -> p (a n)"),
                                          wA[:, 3 * D + 2 + s:3 * D + 3 + s], QSCALE if s == 0 else 1.0,
                                          ALU.add, ALU.mult).then_inc(S["s_q32"], 1)
                    dve.wait_ge(S["s_v"], 2 * l + b + 1)
                    for a in range(2):
                        last = dve.tensor_tensor(
                            vsb[:, 4 * b:4 * b + 4, 4 * a:4 * a + 4, :].rearrange("p g k e -> p k g e"),
                            PS[:, 4 + 2 * b + a, :].rearrange("p (k g e) -> p k g e", k=4, g=4),
                            wV[:, :].rearrange("p (o g e) -> p o g e", o=1, g=4).to_broadcast([P, 4, 4, G * HD]),
                            ALU.add)
                    last.then_inc(S["s_vev"], 1)
                dve.tensor_copy(gcur[:, :, :], gate[:, :, ds(2 * l, 2)].rearrange("p t e -> p e t")).then_inc(s_gc, 1)
                dve.wait_ge(s_gc, l + 1)
                for k in range(P1N):
                    maximum(8 * l, 0, k)
                    if k == 2 * Y0_SLOTS[3] + 2:
                        expert_out(l, 0)
                    if k == 2 * Y1_SLOTS[3] + 2:
                        expert_out(l, 1)

                def stage(u, par, i=None):
                    m = SCH * l + u
                    for k in range(P1N):
                        maximum(8 * l + u + 1, 1 - par, k)
                        for f in range(FT):
                            if i is not None and k == 2 * H_SLOTS[f] + 2:
                                stage_h_out(m, par, f)
                        if i is not None and k == 2 * Y_SLOTS[3] + 2:
                            stage_y_out(m, par, i)
                        if i is None and k == 16:
                            reciprocals(0)

                def reciprocals(b):
                    dve.wait_ge(c_den[b], 16 * l + 16)
                    dve.reciprocal(den[:, b, :], den[:, b, :]).then_inc(S["s_rc"], 1)

                def attention_out(b):
                    half = xr[:, TB * b:TB * b + TB, :]
                    dve.wait_ge(S["s_wo"], 2 * l + b + 1)
                    dve.wait_ge(S["s_bias"], 4 * l + b + 1)
                    dve.tensor_tensor(half, PS[:, 5:7, :].rearrange("p a (t d) -> p (a t) d", d=D), half, ALU.add)\
                        .then_inc(S["s_woev"], 1)
                    dve.wait_ge(S["s_woev"], 2 * l + b + 1)
                    ln_stats(4 * l + 4 + b, b, xr, xc)
                    ln_apply(4 * l + 4 + b, b, xr, xc)

                def normalise(b):
                    dve.wait_ge(c_OT[b], 32 * l + 32)
                    dve.tensor_tensor(OT[:, b, :], OT[:, b, :], rT[:, b, :], ALU.mult).then_inc(S["s_onT"], 1)

                with dve.Fori(0, UN // 2 - 1, 1) as i:
                    stage(2 * i, 0, i)
                    stage(2 * i + 1, 1, i)
                stage(UN - 2, 0)
                normalise(0)
                attention_out(0)
                reciprocals(1)
                normalise(1)
                for b in range(B):
                    dve.wait_ge(S["s_bias"], 4 * l + 3 + b)
                    for c in range(2 + 2 * b, 4 + 2 * b):
                        expert_out(l, c)
                    if b == 0:
                        attention_out(1)

            dve.wait_ge(S["s_yev"], CH * L + CR_YEV)
            for h in range(2):
                ln_stats(4 * L + 2 + h, h, xr, xc)
                ln_apply(4 * L + 2 + h, h, xr, xc)
                dve.wait_ge(S["s_lnxc"], 4 * L + 3 + h)
                o = xc[:, TB * h:TB * h + TB, :]
                for k, (other, op) in enumerate(((finw[:, 0:1, :].to_broadcast([P, TB, D]), ALU.mult),
                                                 (finw[:, 1:2, :].to_broadcast([P, TB, D]), ALU.add),
                                                 (xin[:, TB * h:TB * h + TB, :], ALU.add),
                                                 (acc[:, TB * h:TB * h + TB, :], ALU.add))):
                    dve.tensor_tensor(o, o, other, op).then_inc(S["s_fin"], 1)
                    dve.wait_ge(S["s_fin"], 4 * h + k + 1)


def bf16_bits(a):
    import numpy as np
    w = np.ascontiguousarray(a, np.float32).view(np.uint32).astype(np.uint64)
    return ((w + 0x7FFF + ((w >> 16) & 1)) >> 16).astype(np.uint16)


def bf16_parts(a, n=3):
    import numpy as np
    out = []
    r = np.asarray(a, np.float64)
    for _ in range(n):
        bits = bf16_bits(r)
        out.append(bits)
        r = r - (bits.astype(np.uint32) << 16).view(np.float32).astype(np.float64)
    return out


def constants():
    import numpy as np
    one = bf16_bits(1.0)
    pos = np.arange(P)
    mask = np.zeros((P, 512), np.float32)
    mask[:, 512 - P:] = np.where(pos[None, :] > pos[:, None], -1.0e30, 0.0)
    m2 = np.where(pos[None, :] > pos[:, None], -1.0e30, 0.0)
    kcon = np.zeros((H, 16, T), np.uint16)
    qcon = np.zeros((H, 16, T), np.uint16)
    slopes = (2.0 ** (-0.5 * np.arange(1, H + 1))).astype(np.float32)
    for h in range(H):
        pos = slopes[h].astype(np.float64) * np.arange(T)
        for i, part in enumerate(bf16_parts(pos)):
            kcon[h, i] = part
        for i, part in enumerate(bf16_parts(-pos)):
            qcon[h, 3 + i] = part
        qcon[h, 0:3] = one
        kcon[h, 3:6] = one
        kcon[h, 8:11] = one
    return dict(ident=np.eye(P, dtype=np.float32), identb=bf16_bits(np.eye(P)),
                iota=np.tile(np.arange(E, dtype=np.float32), (P, 1)),
                mask=mask, m2=bf16_bits(m2),
                kcon=kcon.reshape(H, 16, T), qcon=qcon.reshape(H, 16, T))


def kernel(**inputs):
    import numpy as _np
    import concourse.bacc as _bacc
    from concourse import mybir as _mybir
    from concourse.bass_utils import run_bass_kernel_spmd as _run

    a = {k.replace("L0_attn_", "a_").replace("L0_ffn_", "m_"): _np.asarray(v) for k, v in inputs.items()}
    cat = _np.concatenate

    def col(v):
        return v[..., None]

    def tiles(w):
        n = w.shape[0]
        return w.reshape(n, FT, P, D).transpose(0, 2, 1, 3).reshape(n, P, FT * D)

    bi = a["a_in_proj_b"]
    layout = dict(
        x=a["a_x"],
        cA=cat([a["a_in_proj_w"].transpose(0, 2, 1), col(a["a_ln1_w"]), col(a["a_ln1_b"]),
                col(bi[:, 0:D]), col(bi[:, D:2 * D])], axis=2),
        rA=_np.stack([bi[:, 2 * D:], a["a_out_proj_b"], a["a_ffn2_b"]], axis=1),
        cB=cat([a["a_ffn1_w"].transpose(0, 2, 1), tiles(a["a_ffn2_w"].transpose(0, 2, 1)),
                a["a_ffn1_b"].reshape(L, FT, P).transpose(0, 2, 1),
                a["a_out_proj_w"].transpose(0, 2, 1), col(a["a_ln2_w"]), col(a["a_ln2_b"])], axis=2),
        moe=cat([a["m_w1"], tiles(a["m_w2"]), a["m_b1"].reshape(E, FT, P).transpose(0, 2, 1)], axis=2),
        router_w=a["m_router_w"],
        rb_b2=cat([_np.pad(a["m_router_b"], (0, D - E))[None], a["m_b2"]], axis=0),
        fin=_np.stack([a["a_final_w"], a["a_final_b"]]),
    )
    layout.update(constants())
    nc = _bacc.Bacc("TRN2", target_bir_lowering=False, num_devices=1)
    arrays, args = {}, {}
    for name, v in layout.items():
        v = _np.ascontiguousarray(v)
        arrays[f"in_{name}"] = v
        args[name] = nc.dram_tensor(f"in_{name}", v.shape, _mybir.dt.from_np(v.dtype), kind="ExternalInput").ap()
    args["out"] = nc.dram_tensor("out_0", (B, T, D), _mybir.dt.float32, kind="ExternalOutput").ap()
    build(nc, **args)
    r = _run(nc, [arrays], core_ids=[0])
    return r.results[0]["out_0"]
```

```python
from contextlib import ExitStack

import concourse.bass as bass
from concourse import mybir

F32 = mybir.dt.float32
BF16 = mybir.dt.bfloat16
U32 = mybir.dt.uint32
ALU = mybir.AluOpType
ACT = mybir.ActivationFunctionType
AXX = mybir.AxisListType.X
ds = bass.ds

B, T, D, L, H, F, E = 2, 1024, 128, 4, 16, 512, 8
P = 128
HD = D // H
NT = B * T // P
TB = T // P
G = 4
UN = B * H // G
FT = F // P
ROWS = 64
EPS = 1e-5
QSCALE = float(HD) ** -0.5
Q_PARTS = ((slice(0, 3),), (slice(3, 5),), (slice(5, 6),))
K_PARTS = ((slice(0, 1), slice(4, 6)), (slice(1, 4, 2),), (slice(2, 3),))

P1_CHUNKS = [(i, h, c, 512 * c, min(512, P * (i + 1) - 512 * c))
             for i in range(TB) for h in range(G) for c in range(1 + i // 4)]
P1N = len(P1_CHUNKS)
P1L = G * TB // 2
P2_JOBS = [(qh, kt, max(512 * qh, P * kt), 512 * (qh + 1) - max(512 * qh, P * kt))
           for qh, tiles in ((0, (0, 1, 2, 3)), (1, (4, 5, 6, 7, 0, 1, 2, 3))) for kt in tiles]
JOBN = len(P2_JOBS)
DIAG = [kt >= 4 * qh for qh, kt, _, _ in P2_JOBS]
SLOTS = 2 * JOBN
PH = UN // B

CHUNKS = (("E", 0), ("X", 0), ("X", 1), ("E", 1), ("E", 2), ("E", 3))
HBUF = (0, 1, 0, 1, 0, 1)
GELUS = ((0, 10), (0, 22), (1, 7), (2, 10), (2, 17), (3, 10))
H_AT = (((0, 4), (0, 6), (0, 8), (0, 10)), ((0, 18), (0, 19), (0, 20), (0, 21)), ((1, 4), (1, 5), (1, 6), (1, 7)),
        ((2, 4), (2, 6), (2, 8), (2, 10)), ((2, 11), (2, 12), (2, 14), (2, 16)), ((3, 4), (3, 6), (3, 8), (3, 10)))
Y_AT = (((0, 23), (0, 23), (1, 0), (1, 0)), ((1, 8), (1, 8), (1, 9), (1, 9)), ((1, 11), (1, 12), (1, 13), (1, 14)),
        ((2, 18), (2, 18), (2, 19), (2, 19)), ((3, 11), (3, 11), (3, 12), (3, 12)), ((3, 15), (3, 16), (3, 17), (3, 18)))
ON_SCALAR = [(k, f) for k in (0, 3, 5) for f in range(FT)] + [(4, 2), (4, 3)]
RECIP = (0, 5)
NORM = ((0, 9), (0, 10))
STATS2, STATS1 = ((0, 13), (0, 16)), ((1, 10), (1, 15))
FINAL = ((3, 1), (3, 3))
HI, MID = ((1, 19), (1, 23)), ((1, 22), (2, 5))


def plan(ffn, prep, turns=4, chunks=6):
    c = [([(j, 2)], f"turn{j}", 1) for j in range(PH)]
    c += [([(j, (13, 10, 13, 13)[j])], f"turn{j}", 0) for j in range(turns)]
    for k in range(chunks):
        if ffn or CHUNKS[k][0] == "E":
            c += [([H_AT[k][f]], "h", (k, f)) for f in range(FT)] + [(list(Y_AT[k]), "y", k)]
    if ffn:
        c += [([(0, 11)], "wo", 0), ([(0, 12)], "wo", 1), ([(0, 17)], "ln2", 0), ([(0, 22)], "ln2", 1)]
    if prep:
        c += [([(1, s)], kind, 0) for s, kind in ((15, "ln1"), (16, "q"), (17, "k"), (18, "v"))]
        c += [([(1, s)], kind, 1) for s, kind in ((20, "ln1"), (21, "q"), (22, "k"), (23, "v"))]
    return sorted(c, key=lambda e: e[0][0])


FIRST_PLAN, PLAN, LAST_PLAN = plan(False, True), plan(True, True), plan(True, False, turns=3, chunks=5)
START = [((), k, c) for k, c in (("ln1", 0), ("ln1", 1), ("q", 0), ("k", 0), ("q", 1), ("k", 1), ("v", 0), ("v", 1),
                                 ("turn0", 0))]
START_BANK = (7, 5, 7, 5, 7, 5, 7, 5, 7)
START_AFTER = (0, 0, 2, 2, 3, 4, 5, 6, 8)
END = [((), k, c) for k, c in
       [("h", (5, f)) for f in range(FT)] + [("y", 5), ("wo", 0), ("wo", 1), ("ln2", 0), ("ln2", 1)]
       + [("h", (k, f)) for k in (1, 2) for f in range(FT)] + [("y", 1), ("y", 2)]]
END_BANK = (0, 1, 2, 3, 7, 6, 5, 4, 3) + tuple(range(8)) + (0, 1)
END_AFTER = (0,) * 4 + (4,) * 3 + (7, 7) + (9,) * 8 + (17, 17)


def number(contents, kind, which):
    return [e[1:] for e in contents].index((kind, which))


def before(p):
    return len(START) + len(FIRST_PLAN) - len(PLAN) + len(PLAN) * p


def gelus_before(p):
    return UN // B - len(CHUNKS) + len(CHUNKS) * p


def build(nc, x, cA, rA, cB, moe, router_w, rb_b2, fin, ident, identb, iota, mask, m2, kcon, qcon, out):
    with ExitStack() as ctx:
        def sb(name, shape, dt=F32):
            return ctx.enter_context(nc.sbuf_tensor(name, shape, dt))

        def sem(name):
            return ctx.enter_context(nc.semaphore(name))

        def dram(name, shape, dt=F32):
            return nc.dram_tensor(name, shape, dt, kind="Internal").ap()

        PS = ctx.enter_context(nc.psum_tensor("PS", [P, 8, 512], F32))

        kst = dram("kst", [B, H, ROWS, T], BF16)
        qst = dram("qst", [B, H, ROWS, T], BF16)
        onum = dram("onum", [UN, G * HD, T])
        oden = dram("oden", [UN * G, T])
        orec = dram("orec", [UN * G, T])

        idf = sb("idf", [P, P])
        idb = sb("idb", [P, P], BF16)
        io8 = sb("io8", [P, E])
        mkw = sb("mkw", [P, 512])
        mk2 = sb("mk2", [P, P], BF16)
        mhalf = sb("mhalf", [P, 4])
        rw = sb("rw", [P, E])
        rb = sb("rb", [P, E])
        b2e = sb("b2e", [E, D])
        finw = sb("finw", [P, 2, D])
        wA = sb("wA", [P, 3 * D + 4])
        wV = sb("wV", [P, D])
        wR = sb("wR", [P, 2, D])
        wB = sb("wB", [P, D + 2])
        NW = 2 * F + FT
        wE = [sb(f"wE{i}", [P, NW]) for i in range(3)]
        xin = sb("xin", [P, NT, D])
        xr = sb("xr", [P, NT, D])
        acc = sb("acc", [P, NT, D])
        xc = sb("xc", [P, NT, D])
        xn0T = sb("xn0T", [P, B, T])
        xnT = sb("xnT", [P, B, T])
        st = sb("st", [P, 2, 4, 6])
        mv = sb("mv", [P, 2, 4, 2])
        ve = sb("ve", [P, 2, 4])
        rstd = sb("rstd", [P, 2, 4])
        lg = sb("lg", [P, NT, E])
        v8 = sb("v8", [P, NT, E])
        i8 = sb("i8", [P, NT, E], U32)
        i8f = sb("i8f", [P, NT, E])
        gd = sb("gd", [P, NT])
        ge = sb("ge", [P, NT])
        g1 = sb("g1", [P, NT])
        g2 = sb("g2", [P, NT])
        eq = sb("eq", [P, 2, NT, E])
        gate = sb("gate", [P, NT, E])
        gT = sb("gT", [E, NT * P])
        x32 = sb("x32", [P, B, 2, T])
        OT = x32[:, :, 0, :]
        rT = x32[:, :, 1, :]
        parts = sb("parts", [P, 3, 2, T], BF16)
        vsb = sb("vsb", [P, UN, TB, G * HD])
        vbuf = sb("vbuf", [P, 2, TB, G, 32])
        Kop = sb("Kop", [P, 4, 2, T], BF16)
        Qop = sb("Qop", [P, 2, 2, 2, T], BF16)
        mx = sb("mx", [P, 2, TB, G, 2])
        negm = sb("negm", [P, 2, TB, G])
        mres = sb("mres", [P, 2, TB, G])
        mp = sb("mp", [P, 2, TB, G, 3], BF16)
        mrow = sb("mrow", [G * 3, 2, T], BF16)
        PR = sb("PR", [P, 4, 2, 512])
        osb = sb("osb", [P, 2, 512])
        den = sb("den", [P, 2, P])
        hb = sb("hb", [P, 2, FT, 512])

        names = """c_const c_x c_wA c_wB c_con c_out
            s_lnst s_lnag s_lnve s_lnrs s_lnxc s_lnT s_lnev
            s_ms s_lgp s_lg s_v8 s_i8 s_gd s_ge s_g s_gate s_gTp s_gT s_a0p s_a0
            s_hi s_r s_mid s_lo s_bias s_full s_taken s_gelu
            s_p1 s_p1m s_negm s_mpool s_vb
            s_s2 s_exp s_pv s_oev s_rc s_onT s_fin""".split()
        S = {n: sem(n) for n in names}
        c_wE = [sem(f"c_wE{i}") for i in range(2)]
        c_ldl = [sem(f"c_ldl{i}") for i in range(2)]
        c_ldr = [sem(f"c_ldr{i}") for i in range(2)]
        c_m = [[sem(f"c_m{i}{half}") for half in range(2)] for i in range(2)]
        c_o = [sem(f"c_o{i}") for i in range(2)]
        c_od = [sem(f"c_od{i}") for i in range(2)]
        c_stg = [[sem(f"c_stg{b}{half}") for half in range(2)] for b in range(B)]
        passed = sem("passed")
        c_den = [sem(f"c_den{b}") for b in range(B)]
        c_rec = [sem(f"c_rec{b}") for b in range(B)]
        c_OT = [sem(f"c_OT{b}") for b in range(B)]
        ODMA = 16 * 4
        STG = 16 * 7
        CR_EXP, CR_PV, CR_OEV = 2, 2, 1

        block = ctx.enter_context(nc.Block())
        kcov = kcon.bitcast(BF16)
        qcov = qcon.bitcast(BF16)
        xv = x.rearrange("b (t p) d -> p (b t) d", p=P)
        ov = out.rearrange("b (t p) d -> p (b t) d", p=P)
        kun = kst.rearrange("b (g a j) r t -> (b g) (j r) a t", a=2, j=2)
        qun = qst.rearrange("b (g a j) r t -> (b g) (j r) a t", a=2, j=2)
        kfill = kst.rearrange("b h (r k) t -> b (h r) k t", k=8)
        qfill = qst.rearrange("b h (r k) t -> b (h r) k t", k=8)

        MISC = PS[:, 7, :]
        TURN = MISC.bitcast(BF16)[0:3 * G, 0:512]
        x0 = xn0T[:, :, :].rearrange("p b t -> p (b t)")

        def wait_apart(eng, semaphore, value):
            eng.wait_ge(semaphore, value)
            eng.sem_inc(passed, 1)

        def half_tiles(row, c):
            return slice(TB * row + 4 * c, TB * row + 4 * c + 4)


        @block.sync
        def _(sp):
            for h in range(2):
                sp.dma_start(xin[:, TB * h:TB * h + TB, :], xv[:, TB * h:TB * h + TB, :]).then_inc(S["c_x"], 16)
            for dst, src in ((idf[:, :], ident), (idb[:, :], identb.bitcast(BF16)), (io8[:, :], iota), (mkw[:, :], mask),
                             (mk2[:, :], m2.bitcast(BF16)),
                             (rw[:, :], router_w),
                             (rb[:, :], rb_b2[0:1, 0:E].to_broadcast([P, E])),
                             (b2e[:, :], rb_b2[1:1 + E, :]),
                             (finw[:, :, :], fin.unsqueeze(0).to_broadcast([P, 2, D]))):
                sp.dma_start(dst, src).then_inc(S["c_const"], 16)

            def weights_A(q):
                sp.dma_start(wA[:, :], cA[ds(q, 1), :, :].rearrange("l p n -> (l p) n")).then_inc(S["c_wA"], 16)
                sp.dma_start(wV[:, :], rA[ds(q, 1), 0, :].to_broadcast([P, D])).then_inc(S["c_wA"], 16)
                sp.dma_start(wR[:, 0, :], rA[ds(q, 1), 1, :].to_broadcast([P, D])).then_inc(S["c_wA"], 16)

            def weights_B(f):
                sp.dma_start(wB[:, :], cB[ds(f, 1), :, NW:].rearrange("l p n -> (l p) n")).then_inc(S["c_wB"], 16)
                sp.dma_start(wE[2][:, :], cB[ds(f, 1), :, 0:NW].rearrange("l p n -> (l p) n")).then_inc(S["c_wB"], 16)
                sp.dma_start(wR[:, 1, :], rA[ds(f, 1), 2, :].to_broadcast([P, D])).then_inc(S["c_wB"], 16)

            def expert(e, par):
                sp.dma_start(wE[par][:, :], moe[ds(e, 1), :, :].rearrange("l p n -> (l p) n")).then_inc(c_wE[par], 16)

            weights_A(0)
            expert(0, 0)
            for b in range(B):
                for dst, src in ((kfill, kcov), (qfill, qcov)):
                    sp.dma_start(dst[b, :, 6:8, :], src).then_inc(S["c_con"], 16)
            sp.wait_ge(S["c_con"], 64)
            sp.wait_ge(S["s_ms"], 4)

            def load(u, par, kb, half):
                c = (c_ldl, c_ldr)[half][par]
                cols = slice(512 * half, 512 * half + 512)
                for j in range(2):
                    r = slice(ROWS * j, ROWS * j + ROWS)
                    sp.dma_start(Qop[r, par, j, :, cols], qun[u, r, :, cols]).then_inc(c, 16)
                sp.dma_start(Kop[:, kb, :, cols], kun[u, :, :, cols]).then_inc(c, 16)

            def staging(m, row, c, parts_of):
                cols = slice(512 * c, 512 * c + 512)
                for part in parts_of:
                    wait_apart(sp, S[("s_hi", "s_mid", "s_lo")[part]], m + 1)
                    for s, dst in ((0, qfill), (1, kfill)):
                        for blocks in (Q_PARTS, K_PARTS)[s][part]:
                            n = len(range(8)[blocks])
                            sp.dma_start(dst[row, :, blocks, cols],
                                         parts[:, part, s, cols].unsqueeze(1).to_broadcast([P, n, 512]))\
                                .then_inc(c_stg[row][c], 16)

            def minus_max(n, par, half):
                wait_apart(sp, S["s_taken"], n + 1)
                cols = slice(512 * half, 512 * half + 512)
                for h in range(G):
                    r = ROWS * (h % 2) + 8 * 3 + 7
                    sp.dma_start(Qop[r:r + 17:8, par, h % 2, h // 2, cols], mrow[3 * h:3 * h + 3, par, cols])\
                        .then_inc(c_m[par][half], 16)

            def outputs(u, U, qh):
                wait_apart(sp, S["s_oev"], 2 * U + qh + 1 + CR_OEV)
                cols = slice(512 * qh, 512 * qh + 512)
                sp.dma_start(oden[G * u:G * u + G, cols], osb[HD:P:32, qh, :]).then_inc(c_od[qh], 16)
                for h in range(G):
                    sp.dma_start(onum[u, HD * h:HD * h + HD, cols], osb[32 * h:32 * h + HD, qh, :])\
                        .then_inc(c_o[qh], 16)

            def sums_in(p, f, row):
                for qh in range(2):
                    wait_apart(sp, c_od[qh], 64 * p + 16)
                sp.dma_start(den[:, row, :], oden[half_heads(row), :].rearrange("h (c n) -> (h c) n", n=P))\
                    .then_inc(c_den[row], 16)
                for qh in range(2):
                    wait_apart(sp, c_o[qh], ODMA * 4 * p + ODMA)
                sp.dma_start(OT[:, row, :], onum[PH * row:PH * row + PH, :, :].rearrange("u r t -> (u r) t"))\
                    .then_inc(c_OT[row], 16)

            def reciprocals_out(p, row):
                wait_apart(sp, S["s_rc"], p)
                sp.dma_start(orec[half_heads(row), :].rearrange("h (c n) -> (h c) n", n=P), den[:, row, :])\
                    .then_inc(c_rec[row], 16)

            def reciprocals_in(f, row):
                wait_apart(sp, c_rec[row], 16 * f + 16)
                sp.dma_start(rT[:, row, :], orec[half_heads(row), :].unsqueeze(1).to_broadcast([H, HD, T]))\
                    .then_inc(c_OT[row], 16)

            def half_heads(row):
                return slice(H * row, H * row + H)

            def phase(p, b, f, q, base, contents):
                row = 1 - b
                if f is not None:
                    sums_in(p, f, row)
                for j in range(PH):
                    U, u, par = PH * p + j, PH * b + j, j % 2
                    minus_max(base + number(contents, "turn%d" % j, 1), par, 1)
                    if j == 0 and f is not None:
                        reciprocals_out(p, row)
                        if b == 1:
                            wait_apart(sp, S["s_taken"], base)
                            wait_apart(sp, S["s_bias"], 4 * p)
                            weights_B(f)
                        reciprocals_in(f, row)
                    if j == 2 and q is not None:
                        staging(2 * p + 2, row, 0, (0, 1, 2))
                        staging(2 * p + 3, row, 1, (0, 1, 2))
                    outputs(u, U, 0)
                    if j == 0 and q is not None:
                        wait_apart(sp, S["s_taken"], base)
                        expert(p + 1, row)
                        if b == 1:
                            weights_A(q)
                    if j < 3 or q is not None:
                        minus_max(base + number(contents, "turn%d" % j, 0), 1 - par, 0)
                    if j < 2 or q is not None:
                        for half in range(2):
                            wait_apart(sp, S["s_s2"], 24 * U + (8, 24)[half])
                            if j == 2:
                                wait_apart(sp, c_stg[row][half], STG * (q + 1))
                            load((u + 2) % UN, par, (j + 2) % 4, half)
                    outputs(u, U, 1)

            for c in range(2):
                staging(c, 0, c, (0, 1, 2))
            for half in range(2):
                sp.wait_ge(c_stg[0][half], STG)
                for u in range(2):
                    load(u, u, u, half)
            minus_max(number(START, "turn0", 0), 0, 0)
            phase(0, 0, None, 0, len(START), FIRST_PLAN)
            with sp.Fori(0, L - 1, 1) as l:
                phase(2 * l + 1, 1, l, l + 1, before(2 * l + 1), PLAN)
                phase(2 * l + 2, 0, l, l + 1, before(2 * l + 2), PLAN)
            phase(7, 1, L - 1, None, before(7), LAST_PLAN)
            sums_in(8, L - 1, 1)
            reciprocals_out(8, 1)
            reciprocals_in(L - 1, 1)
            for row in range(B):
                for c in range(2):
                    sp.wait_ge(S["s_fin"], 4 * (2 * row + c) + 4)
                    sp.dma_start(ov[:, half_tiles(row, c), :], xc[:, half_tiles(row, c), :]).then_inc(S["c_out"], 16)
            sp.wait_ge(S["c_out"], 64)

        @block.gpsimd
        def _(pool):
            pool.memset(mhalf[:, :], -0.5).then_inc(S["s_ms"], 1)
            pool.memset(vbuf[:, :, :, :, :], 1.0).then_inc(S["s_ms"], 1)
            pool.memset(mx[:, :, :, :, :], -3.0e38).then_inc(S["s_ms"], 1)
            pool.memset(Qop[:, :, :, :, :], 0.0).then_inc(S["s_ms"], 1)
            pool.wait_ge(S["s_ms"], 4)

            def rstd_of(idx, c):
                pool.wait_ge(S["s_lnve"], idx + 1)
                pool.tensor_tensor(rstd[:, c, :], ve[:, c, :], mhalf[:, :], ALU.pow).then_inc(S["s_lnrs"], 1)

            def split_mid(m, row, c):
                cols = slice(512 * c, 512 * c + 512)
                pool.wait_ge(S["s_hi"], m + 1)
                pool.tensor_tensor(x32[:, row, :, cols], x32[:, row, :, cols], parts[:, 0, :, cols],
                                   ALU.subtract).then_inc(S["s_r"], 1)

            def split_lo(m, row, c):
                cols = slice(512 * c, 512 * c + 512)
                pool.wait_ge(S["s_mid"], m + 1)
                pool.tensor_tensor(parts[:, 2, :, cols], x32[:, row, :, cols], parts[:, 1, :, cols],
                                   ALU.subtract).then_inc(S["s_lo"], 1)

            def add_bias(which, idx, row, c):
                pool.wait_ge(S["s_lnxc"], idx + 1)
                tiles = xr[:, half_tiles(row, c), :]
                pool.tensor_tensor(tiles, tiles, wR[:, which:which + 1, :].to_broadcast([P, 4, D]), ALU.add)\
                    .then_inc(S["s_bias"], 1)

            def values(u, par):
                pool.tensor_copy(vbuf[:, par, :, :, 0:HD],
                                 vsb[:, u, :, :].rearrange("p k (g e) -> p k g e", g=G)).then_inc(S["s_vb"], 1)

            def max_parts(U, par, half):
                n = 2 * U + half
                tiles = slice(4 * half, 4 * half + 4)
                wait_apart(pool, S["s_negm"], n + 1)
                pool.tensor_copy(mp[:, par, tiles, :, 0], negm[:, par, tiles, :]).then_inc(S["s_mpool"], 1)
                pool.wait_ge(S["s_mpool"], 4 * n + 1)
                pool.tensor_tensor(mres[:, par, tiles, :], negm[:, par, tiles, :], mp[:, par, tiles, :, 0],
                                   ALU.subtract).then_inc(S["s_mpool"], 1)
                wait_apart(pool, S["s_mpool"], 4 * n + 2)
                pool.tensor_copy(mp[:, par, tiles, :, 1], mres[:, par, tiles, :]).then_inc(S["s_mpool"], 1)
                pool.wait_ge(S["s_mpool"], 4 * n + 3)
                pool.tensor_tensor(mp[:, par, tiles, :, 2], mres[:, par, tiles, :], mp[:, par, tiles, :, 1],
                                   ALU.subtract).then_inc(S["s_mpool"], 1)

            def phase(p, b, f, q, base, contents):
                row = 1 - b
                for j in range(PH):
                    U, par = PH * p + j, j % 2
                    max_parts(U, par, 1)
                    if j == 2 and q is not None:
                        split_lo(2 * p + 2, row, 0)
                        split_mid(2 * p + 3, row, 1)
                    if j < 3 or q is not None:
                        if j == 3:
                            wait_apart(pool, S["s_taken"], base + number(contents, "v", 1) + 1)
                        wait_apart(pool, S["s_pv"], 12 * U + CR_PV)
                        values((PH * b + j + 1) % UN, 1 - par)
                    if j == 2 and q is not None:
                        split_lo(2 * p + 3, row, 1)
                    if j < 3 or q is not None:
                        max_parts(U + 1, 1 - par, 0)
                    if j == 0 and f is not None:
                        for c in range(2):
                            rstd_of(4 * p + 4 + c, c)
                        wait_apart(pool, S["c_wB"], 48 * (f + 1))
                        for c in range(2):
                            add_bias(1, 4 * p + 4 + c, row, c)
                    if j == 1:
                        for c in range(2):
                            rstd_of(4 * p + 6 + c, c)
                            if q is not None:
                                if c == 0:
                                    wait_apart(pool, S["c_wA"], 48 * (q + 1))
                                add_bias(0, 4 * p + 6 + c, row, c)
                        if q is not None:
                            split_mid(2 * p + 2, row, 0)

            for i in range(4):
                rstd_of(i, i % 2)
            split_mid(0, 0, 0)
            split_lo(0, 0, 0)
            for i in range(4, 6):
                rstd_of(i, i % 2)
            split_mid(1, 0, 1)
            split_lo(1, 0, 1)
            pool.wait_ge(S["s_taken"], number(START, "v", 1) + 1)
            values(0, 0)
            pool.wait_ge(S["c_wA"], 48)
            pool.wait_ge(S["s_lnT"], 4)
            for c in range(2):
                add_bias(0, 2 + c, 0, c)
            max_parts(0, 0, 0)
            phase(0, 0, None, 0, len(START), FIRST_PLAN)
            with pool.Fori(0, L - 1, 1) as l:
                phase(2 * l + 1, 1, l, l + 1, before(2 * l + 1), PLAN)
                phase(2 * l + 2, 0, l, l + 1, before(2 * l + 2), PLAN)
            phase(7, 1, L - 1, None, before(7), LAST_PLAN)
            for c in range(2):
                rstd_of(36 + c, c)
            for c in range(2):
                add_bias(1, 36 + c, 1, c)
            for c in range(2):
                rstd_of(38 + c, c)

        @block.scalar
        def _(act):
            act.sem_inc(S["s_exp"], CR_EXP)
            act.sem_inc(S["s_oev"], CR_OEV)

            def norm_out(n, which, layer, row, c, bank=7):
                w, at, loaded = ((wA, 3 * D, S["c_wA"]), (wB, D, S["c_wB"]))[which - 1]
                wait_apart(act, loaded, 48 * (layer + 1))
                act.wait_ge(S["s_full"], n + 1)
                act.activation(xnT[:, row, 512 * c:512 * c + 512], PS[:, bank, :], ACT.Identity, scale=w[:, at:at + 1],
                               bias=w[:, at + 1:at + 2]).then_inc(S["s_taken"], 1)

            def x0_out(k):
                act.wait_ge(S["s_lnT"], k + 1)
                act.activation(x0[:, 512 * k:512 * k + 512], PS[:, k, :], ACT.Copy).then_inc(S["s_lnev"], 1)

            def turn_out(n, U, par, half):
                act.wait_ge(S["s_full"], n + 1)
                act.activation(mrow[:, par, 512 * half:512 * half + 512], TURN, ACT.Copy).then_inc(S["s_taken"], 1)

            def h_out(n, k, f, b):
                act.wait_ge(S["s_full"], n + 1)
                w = wE[b if CHUNKS[k][0] == "E" else 2]
                act.activation(hb[:, HBUF[k], f, :], MISC, ACT.Identity, bias=w[:, 2 * F + f:2 * F + f + 1])\
                    .then_inc(S["s_taken"], 1)

            def gelu(chunk, taken):
                act.wait_ge(S["s_taken"], taken)
                act.activation(hb[:, HBUF[chunk], :, :], hb[:, HBUF[chunk], :, :], ACT.Gelu).then_inc(S["s_gelu"], 1)

            def split_hi(m, row, c, taken):
                cols = slice(512 * c, 512 * c + 512)
                act.wait_ge(S["s_taken"], taken)
                act.activation(parts[:, 0, :, cols], x32[:, row, :, cols], ACT.Copy).then_inc(S["s_hi"], 1)

            def split_mid(m, row, c):
                cols = slice(512 * c, 512 * c + 512)
                act.wait_ge(S["s_r"], m + 1)
                act.activation(parts[:, 1, :, cols], x32[:, row, :, cols], ACT.Copy).then_inc(S["s_mid"], 1)

            def exps(U, c):
                t, a = c // 2, c % 2
                n = P2_JOBS[t][3]
                act.wait_ge(S["s_s2"], 24 * U + c + 1)
                if a == 0:
                    act.wait_ge(S["s_pv"], 12 * U + t - 1 + CR_PV)
                act.activation(PR[:, c % 4, :, 0:n], PS[:, 2 * (c % 2):2 * (c % 2) + 2, 0:n], ACT.Exp)\
                    .then_inc(S["s_exp"], 1)

            def sums_out(U, qh):
                act.wait_ge(S["s_pv"], 12 * U + (4, 12)[qh] + CR_PV)
                act.wait_ge(c_od[qh], 16 * U + 16)
                act.wait_ge(c_o[qh], ODMA * U + ODMA)
                act.activation(osb[:, qh, :], PS[:, 4, :], ACT.Copy).then_inc(S["s_oev"], 1)

            def phase(p, b, f, q, base, contents):
                row = 1 - b
                for j in range(PH):
                    U, par = PH * p + j, j % 2
                    for s in range(SLOTS):
                        exps(U, s)
                        if s == 0 and not (f is None and j == 0):
                            sums_out(U - 1, 1)
                        if s == 9:
                            sums_out(U, 0)
                        for n, (spots, kind, which) in enumerate(contents):
                            if (j, s) in spots:
                                if kind[:4] == "turn" and which == 1:
                                    turn_out(base + n, U, par, 1)
                                if kind[:4] == "turn" and which == 0:
                                    turn_out(base + n, U + 1, 1 - par, 0)
                                if kind == "h" and which in ON_SCALAR:
                                    h_out(base + n, which[0], which[1], b)
                                if kind == "ln2":
                                    norm_out(base + n, 2, f, row, which)
                                if kind == "ln1":
                                    norm_out(base + n, 1, q, row, which)
                        for k in range(6):
                            if GELUS[k] == (j, s) and ("y", k) in [e[1:] for e in contents]:
                                gelu(k, base + number(contents, "h", (k, 3)) + 1)
                        for c in range(2):
                            if q is not None and HI[c] == (j, s):
                                split_hi(2 * p + 2 + c, row, c, base + number(contents, "k", c) + 1)
                            if q is not None and MID[c] == (j, s):
                                split_mid(2 * p + 2 + c, row, c)

            for c in range(2):
                n = number(START, "ln1", c)
                norm_out(n, 1, 0, 0, c, START_BANK[n])
            for c in range(2):
                split_hi(c, 0, c, number(START, "k", c) + 1)
                if c == 1:
                    for k in range(2):
                        x0_out(k)
                split_mid(c, 0, c)
            for k in range(2, 4):
                x0_out(k)
            act.wait_ge(S["s_gd"], 1)
            act.activation(ge[:, :], gd[:, :], ACT.Exp).then_inc(S["s_ge"], 1)
            act.wait_ge(S["s_gTp"], 1)
            act.activation(gT[:, :], PS[0:E, 0:4, :], ACT.Copy).then_inc(S["s_gT"], 1)
            turn_out(number(START, "turn0", 0), 0, 0, 0)
            phase(0, 0, None, 0, len(START), FIRST_PLAN)
            with act.Fori(0, L - 1, 1) as l:
                phase(2 * l + 1, 1, l, l + 1, before(2 * l + 1), PLAN)
                phase(2 * l + 2, 0, l, l + 1, before(2 * l + 2), PLAN)
            phase(7, 1, L - 1, None, before(7), LAST_PLAN)
            sums_out(L * UN - 1, 1)
            base = before(7) + len(LAST_PLAN)
            gelu(5, base + number(END, "h", (5, 3)) + 1)
            for c in range(2):
                n = number(END, "ln2", c)
                norm_out(base + n, 2, L - 1, 1, c, END_BANK[n])
            for k in (1, 2):
                gelu(k, base + number(END, "h", (k, 3)) + 1)

        @block.tensor
        def _(pe):
            pe.sem_inc(S["s_pv"], CR_PV)

            def taken(n):
                if not (isinstance(n, int) and n == 0):
                    pe.wait_ge(S["s_taken"], n)

            def turn(n, U, par, half):
                pe.wait_ge(S["s_mpool"], 4 * (2 * U + half) + 4)
                taken(n)
                for i in range(4):
                    last = pe.transpose(TURN[:, P * i:P * i + P],
                                        mp[:, par, 4 * half + i, :, :].rearrange("p g c -> p (g c)"), idb[:, :])
                last.then_inc(S["s_full"], 1)

            def norm_turn(n, idx, row, c, bank=7):
                pe.wait_ge(S["s_lnxc"], idx + 1)
                taken(n)
                for t in range(4):
                    last = pe.transpose(PS[:, bank, P * t:P * t + P], xc[:, TB * row + 4 * c + t, :], idf[:, :])
                last.then_inc(S["s_full"], 1)

            def h_piece(n, k, i, f, b, row, bank=7):
                what, c = CHUNKS[k]
                w = wE[b if what == "E" else 2]
                src = x0[:, 512 * c:512 * c + 512] if what == "E" else xnT[:, row, 512 * c:512 * c + 512]
                if f == 0:
                    if what == "E":
                        wait_apart(pe, c_wE[b], 16 * (i + 1))
                    else:
                        wait_apart(pe, S["c_wB"], 48 * (i + 1))
                taken(n)
                pe.matmul(PS[:, bank, :], w[:, P * f:P * f + P], src, start=True, stop=True).then_inc(S["s_full"], 1)

            def y_piece(n, k, g, b, j, bank=7):
                w = wE[b if CHUNKS[k][0] == "E" else 2]
                if j == 0:
                    wait_apart(pe, S["s_gelu"], g + 1)
                    taken(n)
                for f in range(FT):
                    last = pe.matmul(PS[:, bank, P * j:P * j + P], hb[:, HBUF[k], f, P * j:P * j + P],
                                     w[:, F + P * f:F + P * f + P], start=(f == 0), stop=(f == FT - 1))
                if j == 3:
                    last.then_inc(S["s_full"], 1)

            def attention_out(n, m, f, row, c, bank=7):
                wait_apart(pe, S["c_wB"], 48 * (f + 1))
                pe.wait_ge(S["s_onT"], m + 1)
                taken(n)
                for t in range(4):
                    last = pe.matmul(PS[:, bank, P * t:P * t + P], OT[:, row, P * (4 * c + t):P * (4 * c + t) + P],
                                     wB[:, 0:D], start=True, stop=True)
                last.then_inc(S["s_full"], 1)

            def project(n, s, q, row, c, bank=7):
                if s == 0:
                    wait_apart(pe, S["c_wA"], 48 * (q + 1))
                taken(n)
                if s < 2:
                    last = pe.matmul(PS[:, bank, :], wA[:, D * s:D * s + D], xnT[:, row, 512 * c:512 * c + 512],
                                     start=True, stop=True)
                else:
                    for t in range(4):
                        last = pe.matmul(PS[:, bank, P * t:P * t + P], xnT[:, row, P * (4 * c + t):P * (4 * c + t) + P],
                                         wA[:, 2 * D:3 * D], start=True, stop=True)
                last.then_inc(S["s_full"], 1)

            def p1_chunk(U, par, kb, nth, k, first=False):
                i, h, c, k0, n = P1_CHUNKS[k]
                if k == 0:
                    pe.wait_ge(c_ldl[par], 48 * (nth + 1))
                if k == P1L:
                    pe.wait_ge(c_ldr[par], 48 * (nth + 1))
                if k >= 2 or not first:
                    pe.wait_ge(S["s_p1m"], P1N * U + k - 1)
                pe.matmul(PS[:, 5 + k % 2, 0:n], Qop[:, par, h % 2, h // 2, P * i:P * i + P],
                          Kop[:, kb, h // 2, k0:k0 + n], start=True, stop=True).then_inc(S["s_p1"], 1)

            def p2_pair(U, par, kb, nth, c):
                t, a = c // 2, c % 2
                qh, kt, q0, n = P2_JOBS[t]
                if c == 0 or c == 8:
                    pe.wait_ge(c_m[par][c // 8], 64 * (nth + 1))
                pe.wait_ge(S["s_exp"], 24 * U + c - 1 + CR_EXP)
                for j in range(2):
                    bank = PS[:, 2 * (c % 2) + j, :]
                    last = pe.matmul(bank[:, 0:n], Kop[:, kb, a, P * kt:P * kt + P], Qop[:, par, j, a, q0:q0 + n],
                                     start=True, stop=not DIAG[t])
                    if DIAG[t]:
                        last = pe.matmul(bank[:, 0:P], mk2[:, :], idb[:, :], start=False, stop=True)
                last.then_inc(S["s_s2"], 1)

            def p2_values(U, par, t):
                qh, kt, q0, n = P2_JOBS[t]
                if t == 0:
                    pe.wait_ge(S["s_vb"], U + 1)
                if t in (0, 4):
                    pe.wait_ge(S["s_oev"], 2 * U + qh + CR_OEV)
                pe.wait_ge(S["s_exp"], 24 * U + 2 * t + 2 + CR_EXP)
                for h in range(G):
                    last = pe.matmul(PS[32 * h:32 * h + 32, 4, q0 - 512 * qh:512], vbuf[:, par, kt, h, :],
                                     PR[:, 2 * (t % 2) + h // 2, h % 2, 0:n],
                                     start=t in (0, 4), stop=t in (3, 11))
                last.then_inc(S["s_pv"], 1)

            def phase(p, b, f, q, base, contents):
                row = 1 - b
                place = f if b == 1 else q
                g0 = 0 if f is None else gelus_before(p)
                done = [k for k in range(6) if CHUNKS[k][0] == "E" or f is not None]
                for j in range(PH):
                    U, par, nth = PH * p + j, j % 2, 2 * p + j // 2
                    more = j < 3 or q is not None
                    for s in range(SLOTS):
                        if more:
                            p1_chunk(U + 1, 1 - par, (j + 1) % 4, nth + par, 2 * s)
                        p2_pair(U, par, j, nth, s)
                        for n, (spots, kind, which) in enumerate(contents):
                            if (j, s) in spots:
                                if kind[:4] == "turn" and which == 1:
                                    turn(base + n, U, par, 1)
                                if kind[:4] == "turn" and which == 0:
                                    turn(base + n, U + 1, 1 - par, 0)
                                if kind == "h":
                                    h_piece(base + n, which[0], place if CHUNKS[which[0]][0] == "E" else f,
                                            which[1], b, row)
                                if kind == "wo":
                                    attention_out(base + n, 2 * p - 2 + which, f, row, which)
                                if kind == "ln2":
                                    norm_turn(base + n, 4 * p + 4 + which, row, which)
                                if kind == "ln1":
                                    norm_turn(base + n, 4 * p + 6 + which, row, which)
                                if kind in ("q", "k", "v"):
                                    project(base + n, "qkv".index(kind), q, row, which)
                                if kind == "y":
                                    for t in range(4):
                                        if spots[t] == (j, s):
                                            y_piece(base + n, which, g0 + done.index(which), b, t)
                        if more:
                            p1_chunk(U + 1, 1 - par, (j + 1) % 4, nth + par, 2 * s + 1)
                        if s == 0 and not (f is None and j == 0):
                            p2_values(U - 1, 1 - par, JOBN - 1)
                        if s % 2 == 1 and s >= 3:
                            p2_values(U, par, s // 2 - 1)

            pe.wait_ge(S["c_const"], 16 * 9)
            for n, (_, kind, c) in enumerate(START):
                if kind == "ln1":
                    norm_turn(START_AFTER[n], 2 + c, 0, c, START_BANK[n])
                if kind in ("q", "k", "v"):
                    project(START_AFTER[n], "qkv".index(kind), 0, 0, c, START_BANK[n])
            for k in range(4):
                pe.wait_ge(S["s_lnxc"], (1, 2, 5, 6)[k])
                for t in range(4):
                    last = pe.transpose(PS[:, k, P * t:P * t + P], xr[:, 4 * k + t, :], idf[:, :])
                last.then_inc(S["s_lnT"], 1)
            pe.wait_ge(S["s_lnev"], 4)
            for t in range(NT):
                last = pe.matmul(PS[:, 4, E * t:E * t + E], x0[:, P * t:P * t + P], rw[:, :], start=True, stop=True)
            last.then_inc(S["s_lgp"], 1)
            pe.wait_ge(S["s_taken"], 8)
            for k in range(P1N):
                p1_chunk(0, 0, 0, 0, k, first=True)
                if k == 8:
                    pe.wait_ge(S["s_gate"], 1)
                    for t in range(NT):
                        last = pe.transpose(PS[0:E, t // 4, P * (t % 4):P * (t % 4) + P], gate[:, t, :], idf[:, :])
                    last.then_inc(S["s_gTp"], 1)
                if k == 20:
                    turn(number(START, "turn0", 0), 0, 0, 0)
                if k == 24:
                    pe.wait_ge(S["s_gT"], 1)
                if k >= 24 and k % 6 == 0:
                    j = (k - 24) // 6
                    for t in range(4 * j, 4 * j + 4):
                        last = pe.matmul(PS[:, j, P * (t % 4):P * (t % 4) + P], gT[:, P * t:P * t + P], b2e[:, :],
                                         start=True, stop=True)
                    last.then_inc(S["s_a0p"], 1)
            pe.wait_ge(S["s_a0"], 4)
            phase(0, 0, None, 0, len(START), FIRST_PLAN)
            with pe.Fori(0, L - 1, 1) as l:
                phase(2 * l + 1, 1, l, l + 1, before(2 * l + 1), PLAN)
                phase(2 * l + 2, 0, l, l + 1, before(2 * l + 2), PLAN)
            phase(7, 1, L - 1, None, before(7), LAST_PLAN)
            p2_values(L * UN - 1, 1, JOBN - 1)
            base = before(7) + len(LAST_PLAN)
            for n, (_, kind, which) in enumerate(END):
                after, bank = base + END_AFTER[n], END_BANK[n]
                if n == 0:
                    pe.wait_ge(S["s_oev"], 2 * L * UN + CR_OEV)
                    pe.wait_ge(S["s_p1m"], L * UN * P1N)
                if kind == "wo":
                    attention_out(after, 14 + which, L - 1, 1, which, bank)
                if kind == "ln2":
                    norm_turn(after, 36 + which, 1, which, bank)
                if kind == "h":
                    h_piece(after, which[0], L - 1, which[1], 1, 1, bank)
                if kind == "y":
                    for j in range(4):
                        y_piece(after, which, gelus_before(8) + (5, 1, 2).index(which) - 1, 1, j, bank)

        @block.vector
        def _(dve):
            for qh in range(2):
                dve.sem_inc(c_o[qh], ODMA)
                dve.sem_inc(c_od[qh], 16)

            def ln_sums(idx, row, c, src):
                for t in range(4):
                    last = dve.bn_stats(st[:, c, t, :], src[:, TB * row + 4 * c + t, :])
                last.then_inc(S["s_lnst"], 1)

            def ln_mean(idx, c):
                wait_apart(dve, S["s_lnst"], idx + 1)
                for t in range(4):
                    last = dve.bn_aggr(mv[:, c, t, :], st[:, c, t, :])
                last.then_inc(S["s_lnag"], 1)

            def ln_var(idx, c):
                dve.wait_ge(S["s_lnag"], idx + 1)
                dve.tensor_scalar(ve[:, c, :], mv[:, c, :, 1], EPS, None, ALU.add).then_inc(S["s_lnve"], 1)

            def ln_stats(idx, row, c, src):
                ln_sums(idx, row, c, src)
                ln_mean(idx, c)
                ln_var(idx, c)

            def ln_apply(idx, row, c, src, dst, tiles=(0, 1, 2, 3)):
                if tiles[0] == 0:
                    dve.wait_ge(S["s_lnrs"], idx + 1)
                for t in tiles:
                    tile = TB * row + 4 * c + t
                    last = dve.tensor_scalar(dst[:, tile, :], src[:, tile, :], mv[:, c, t, 0:1],
                                             rstd[:, c, t:t + 1], ALU.subtract, ALU.mult)
                if tiles[-1] == 3:
                    last.then_inc(S["s_lnxc"], 1)

            def h_out(n, k, f, b, bank):
                dve.wait_ge(S["s_full"], n + 1)
                w = wE[b if CHUNKS[k][0] == "E" else 2]
                dve.tensor_scalar(hb[:, HBUF[k], f, :], PS[:, bank, :], w[:, 2 * F + f:2 * F + f + 1], None, ALU.add)\
                    .then_inc(S["s_taken"], 1)

            def y_out(n, k, p, biases, row, bank):
                what, c = CHUNKS[k]
                if what == "E":
                    dve.wait_ge(S["s_full"], n + 1)
                    for j in range(4):
                        t = 4 * c + j
                        last = dve.scalar_tensor_tensor(out=acc[:, t, :], in0=PS[:, bank, P * j:P * j + P],
                                                        scalar=gate[:, t, ds(p, 1)], in1=acc[:, t, :],
                                                        op0=ALU.mult, op1=ALU.add)
                else:
                    wait_apart(dve, S["s_bias"], biases + c + 1)
                    dve.wait_ge(S["s_full"], n + 1)
                    tiles = xr[:, half_tiles(row, c), :]
                    last = dve.tensor_tensor(tiles, PS[:, bank, :].rearrange("p (t d) -> p t d", t=4), tiles, ALU.add)
                last.then_inc(S["s_taken"], 1)

            def wo_out(n, biases, row, c, bank):
                wait_apart(dve, S["s_bias"], biases)
                dve.wait_ge(S["s_full"], n + 1)
                tiles = xr[:, half_tiles(row, c), :]
                dve.tensor_tensor(tiles, PS[:, bank, :].rearrange("p (t d) -> p t d", t=4), tiles, ALU.add)\
                    .then_inc(S["s_taken"], 1)

            def qk_out(n, s, row, c, bank):
                dve.wait_ge(S["s_full"], n + 1)
                dve.tensor_scalar(x32[:, row, s, 512 * c:512 * c + 512], PS[:, bank, :], wA[:, 3 * D + 2 + s:3 * D + 3 + s],
                                  QSCALE if s == 0 else 1.0, ALU.add, ALU.mult).then_inc(S["s_taken"], 1)

            def v_out(n, row, c, bank):
                dve.wait_ge(S["s_full"], n + 1)
                dve.tensor_tensor(vsb[:, 4 * row:4 * row + 4, 4 * c:4 * c + 4, :].rearrange("p g k e -> p k g e"),
                                  PS[:, bank, :].rearrange("p (k g e) -> p k g e", k=4, g=4),
                                  wV[:, :].rearrange("p (o g e) -> p o g e", o=1, g=4).to_broadcast([P, 4, 4, G * HD]),
                                  ALU.add).then_inc(S["s_taken"], 1)

            def out_of_bank(n, kind, which, p, biases, b, row, bank=7):
                if kind == "h":
                    h_out(n, which[0], which[1], b, bank)
                if kind == "y":
                    y_out(n, which, p, biases, row, bank)
                if kind == "wo":
                    wo_out(n, biases, row, which, bank)
                if kind in ("q", "k"):
                    qk_out(n, "qk".index(kind), row, which, bank)
                if kind == "v":
                    v_out(n, row, which, bank)

            def reciprocals(f, row):
                dve.wait_ge(c_den[row], 16 * f + 16)
                dve.reciprocal(den[:, row, :], den[:, row, :]).then_inc(S["s_rc"], 1)

            def normalise(f, row, c):
                cols = slice(512 * c, 512 * c + 512)
                dve.wait_ge(c_OT[row], 32 * f + 32)
                dve.tensor_tensor(OT[:, row, cols], OT[:, row, cols], rT[:, row, cols], ALU.mult)\
                    .then_inc(S["s_onT"], 1)

            def final(row, c, idx):
                dve.wait_ge(S["s_lnxc"], idx + 1)
                o = xc[:, half_tiles(row, c), :]
                for k, (other, op) in enumerate(((finw[:, 0:1, :].to_broadcast([P, 4, D]), ALU.mult),
                                                 (finw[:, 1:2, :].to_broadcast([P, 4, D]), ALU.add),
                                                 (xin[:, half_tiles(row, c), :], ALU.add),
                                                 (acc[:, half_tiles(row, c), :], ALU.add))):
                    dve.tensor_tensor(o, o, other, op).then_inc(S["s_fin"], 1)
                    dve.wait_ge(S["s_fin"], 4 * (2 * row + c) + k + 1)

            def maximum(U, par, k):
                i, h, c, k0, n = P1_CHUNKS[k]
                chunk = PS[:, 5 + k % 2, 0:n]
                if k0 + n == P * (i + 1):
                    wait_apart(dve, S["s_p1"], P1N * U + k + 1)
                    dve.tensor_tensor_reduce(chunk, chunk, mkw[:, 512 - n:512], 1.0, -3.0e38, ALU.add, ALU.max,
                                             mx[:, par, i, h, c:c + 1]).then_inc(S["s_p1m"], 1)
                else:
                    dve.wait_ge(S["s_p1"], P1N * U + k + 1)
                    dve.tensor_reduce(mx[:, par, i, h, c:c + 1], chunk, AXX, ALU.max).then_inc(S["s_p1m"], 1)
                if k == P1L - 1 or k == P1N - 1:
                    tiles = slice(0, 4) if k == P1L - 1 else slice(4, 8)
                    dve.wait_ge(S["s_p1m"], P1N * U + k + 1)
                    dve.tensor_reduce(negm[:, par, tiles, :], mx[:, par, tiles, :, :], AXX, ALU.max, negate=True)\
                        .then_inc(S["s_negm"], 1)

            def ln_step(idx, row, c, first, now, ready):
                (j, k), (j0, s0) = now, first
                if (j, k) == (j0, 2 * s0 + 1):
                    if ready is not None:
                        wait_apart(dve, S["s_taken"], ready)
                    ln_sums(idx, row, c, xr)
                if (j, k) == (j0, 2 * s0 + 2):
                    ln_mean(idx, c)
                if (j, k) == (j0, 2 * s0 + 3):
                    ln_var(idx, c)
                if (j, k) == (j0, 2 * s0 + 5):
                    ln_apply(idx, row, c, xr, xc, (0, 1))
                if (j, k) == (j0, 2 * s0 + 7):
                    ln_apply(idx, row, c, xr, xc, (2, 3))

            def phase(p, b, f, q, base, contents):
                row = 1 - b
                for j in range(PH):
                    U, par = PH * p + j, j % 2
                    for k in range(P1N):
                        if j < 3 or q is not None:
                            maximum(U + 1, 1 - par, k)
                        now = (j, k // 2)
                        if k % 2 == 0:
                            for n, (spots, kind, which) in enumerate(contents):
                                if spots[-1] == now and not (kind == "h" and which in ON_SCALAR):
                                    out_of_bank(base + n, kind, which, p, 4 * p, b, row)
                        for c in range(2):
                            if f is not None:
                                ln_step(4 * p + 4 + c, row, c, STATS2[c], (j, k), base + number(contents, "wo", c) + 1)
                            ln_step(4 * p + 6 + c, row, c, STATS1[c], (j, k),
                                    None if f is None else base + number(contents, "y", 1 + c) + 1)
                        if k % 2 == 0:
                            continue
                        if f is not None and now == RECIP:
                            reciprocals(f, row)
                        for c in range(2):
                            if f is not None and now == NORM[c]:
                                normalise(f, row, c)
                            if q is None and now == FINAL[c]:
                                final(row, c, 4 * p + 6 + c)

            dve.wait_ge(S["c_x"], 16 * 2)
            for c in range(2):
                ln_stats(c, 0, c, xin)
            for c in range(2):
                ln_apply(c, 0, c, xin, xr)
            for c in range(2):
                dve.wait_ge(S["s_lnxc"], c + 1)
                ln_stats(2 + c, 0, c, xr)
            for c in range(2):
                ln_apply(2 + c, 0, c, xr, xc)
            for n, (_, kind, c) in enumerate(START):
                out_of_bank(n, kind, c, 0, 0, 0, 0, START_BANK[n])
            for c in range(2):
                ln_stats(4 + c, 1, c, xin)
            for c in range(2):
                ln_apply(4 + c, 1, c, xin, xr)
            dve.wait_ge(S["c_const"], 16 * 9)
            dve.wait_ge(S["s_lgp"], 1)
            dve.tensor_tensor(lg[:, :, :], PS[:, 4, 0:NT * E].rearrange("p (t e) -> p t e", e=E),
                              rb[:, :].unsqueeze(1).to_broadcast([P, NT, E]), ALU.add).then_inc(S["s_lg"], 1)
            dve.wait_ge(S["s_lg"], 1)
            for t in range(NT):
                last = dve.max(v8[:, t, :], lg[:, t, :])
            last.then_inc(S["s_v8"], 1)
            dve.wait_ge(S["s_v8"], 1)
            dve.tensor_tensor(gd[:, :], v8[:, :, 1], v8[:, :, 0], ALU.subtract).then_inc(S["s_gd"], 1)
            for t in range(NT):
                last = dve.max_index(i8[:, t, :], v8[:, t, :], lg[:, t, :])
            last.then_inc(S["s_i8"], 1)
            dve.wait_ge(S["s_i8"], 1)
            dve.tensor_copy(i8f[:, :, :], i8[:, :, :]).then_inc(S["s_g"], 1)
            dve.wait_ge(S["s_ge"], 1)
            dve.tensor_scalar(gd[:, :], ge[:, :], 1.0, None, ALU.add).then_inc(S["s_g"], 1)
            dve.wait_ge(S["s_g"], 2)
            dve.reciprocal(g1[:, :], gd[:, :]).then_inc(S["s_g"], 1)
            for k in range(2):
                dve.tensor_tensor(eq[:, k, :, :], io8[:, :].unsqueeze(1).to_broadcast([P, NT, E]),
                                  i8f[:, :, k:k + 1].to_broadcast([P, NT, E]), ALU.is_equal).then_inc(S["s_g"], 1)
            dve.wait_ge(S["s_g"], 5)
            dve.tensor_tensor(g2[:, :], ge[:, :], g1[:, :], ALU.mult).then_inc(S["s_g"], 1)
            dve.tensor_tensor(eq[:, 0, :, :], eq[:, 0, :, :], g1[:, :].unsqueeze(2).to_broadcast([P, NT, E]), ALU.mult)\
                .then_inc(S["s_g"], 1)
            dve.wait_ge(S["s_g"], 7)
            dve.tensor_tensor(eq[:, 1, :, :], eq[:, 1, :, :], g2[:, :].unsqueeze(2).to_broadcast([P, NT, E]), ALU.mult)\
                .then_inc(S["s_g"], 1)
            dve.wait_ge(S["s_g"], 8)
            dve.tensor_tensor(gate[:, :, :], eq[:, 0, :, :], eq[:, 1, :, :], ALU.add).then_inc(S["s_gate"], 1)
            dve.wait_ge(S["s_ms"], 4)
            for k in range(P1N):
                maximum(0, 0, k)
                if k >= 26 and k % 6 == 2:
                    j = (k - 26) // 6
                    dve.wait_ge(S["s_a0p"], j + 1)
                    dve.tensor_copy(acc[:, 4 * j:4 * j + 4, :], PS[:, j, :].rearrange("p (t d) -> p t d", d=D))\
                        .then_inc(S["s_a0"], 1)
            phase(0, 0, None, 0, len(START), FIRST_PLAN)
            with dve.Fori(0, L - 1, 1) as l:
                phase(2 * l + 1, 1, l, l + 1, before(2 * l + 1), PLAN)
                phase(2 * l + 2, 0, l, l + 1, before(2 * l + 2), PLAN)
            phase(7, 1, L - 1, None, before(7), LAST_PLAN)
            base = before(7) + len(LAST_PLAN)
            for n, (_, kind, which) in enumerate(END):
                if (kind, which) == ("wo", 0):
                    for c in range(2):
                        normalise(L - 1, 1, c)
                out_of_bank(base + n, kind, which, 7, 4 * 7 + 2, 1, 1, END_BANK[n])
                if (kind, which) == ("h", (5, 3)):
                    reciprocals(L - 1, 1)
                if (kind, which) == ("wo", 1):
                    for c in range(2):
                        dve.wait_ge(S["s_taken"], base + number(END, "wo", c) + 1)
                        ln_stats(36 + c, 1, c, xr)
                    for c in range(2):
                        ln_apply(36 + c, 1, c, xr, xc)
            for c in range(2):
                dve.wait_ge(S["s_taken"], base + number(END, "y", 1 + c) + 1)
                ln_stats(38 + c, 1, c, xr)
            for c in range(2):
                ln_apply(38 + c, 1, c, xr, xc)
                final(1, c, 38 + c)


def bf16_bits(a):
    import numpy as np
    w = np.ascontiguousarray(a, np.float32).view(np.uint32).astype(np.uint64)
    return ((w + 0x7FFF + ((w >> 16) & 1)) >> 16).astype(np.uint16)


def bf16_parts(a, n=3):
    import numpy as np
    out = []
    r = np.asarray(a, np.float64)
    for _ in range(n):
        bits = bf16_bits(r)
        out.append(bits)
        r = r - (bits.astype(np.uint32) << 16).view(np.float32).astype(np.float64)
    return out


def constants():
    import numpy as np
    one = bf16_bits(1.0)
    pos = np.arange(P)
    mask = np.zeros((P, 512), np.float32)
    mask[:, 512 - P:] = np.where(pos[None, :] > pos[:, None], -1.0e30, 0.0)
    m2 = np.where(pos[None, :] > pos[:, None], -1.0e30, 0.0)
    kcon = np.zeros((H, 8, 2, T), np.uint16)
    qcon = np.zeros((H, 8, 2, T), np.uint16)
    slopes = (2.0 ** (-0.5 * np.arange(1, H + 1))).astype(np.float32)
    for h in range(H):
        pos = slopes[h].astype(np.float64) * np.arange(T)
        for i, part in enumerate(bf16_parts(pos)):
            kcon[h, i, 0] = part
        for i, part in enumerate(bf16_parts(-pos)):
            qcon[h, i, 1] = part
        qcon[h, 0:3, 0] = one
        kcon[h, 0:3, 1] = one
        kcon[h, 3:6, 1] = one
    return dict(ident=np.eye(P, dtype=np.float32), identb=bf16_bits(np.eye(P)),
                iota=np.tile(np.arange(E, dtype=np.float32), (P, 1)),
                mask=mask, m2=bf16_bits(m2),
                kcon=kcon.reshape(H * 8, 2, T), qcon=qcon.reshape(H * 8, 2, T))


def kernel(**inputs):
    import numpy as _np
    import concourse.bacc as _bacc
    from concourse import mybir as _mybir
    from concourse.bass_utils import run_bass_kernel_spmd as _run

    a = {k.replace("L0_attn_", "a_").replace("L0_ffn_", "m_"): _np.asarray(v) for k, v in inputs.items()}
    cat = _np.concatenate

    def col(v):
        return v[..., None]

    def tiles(w):
        n = w.shape[0]
        return w.reshape(n, FT, P, D).transpose(0, 2, 1, 3).reshape(n, P, FT * D)

    bi = a["a_in_proj_b"]
    layout = dict(
        x=a["a_x"],
        cA=cat([a["a_in_proj_w"].transpose(0, 2, 1), col(a["a_ln1_w"]), col(a["a_ln1_b"]),
                col(bi[:, 0:D]), col(bi[:, D:2 * D])], axis=2),
        rA=_np.stack([bi[:, 2 * D:], a["a_out_proj_b"], a["a_ffn2_b"]], axis=1),
        cB=cat([a["a_ffn1_w"].transpose(0, 2, 1), tiles(a["a_ffn2_w"].transpose(0, 2, 1)),
                a["a_ffn1_b"].reshape(L, FT, P).transpose(0, 2, 1),
                a["a_out_proj_w"].transpose(0, 2, 1), col(a["a_ln2_w"]), col(a["a_ln2_b"])], axis=2),
        moe=cat([a["m_w1"], tiles(a["m_w2"]), a["m_b1"].reshape(E, FT, P).transpose(0, 2, 1)], axis=2),
        router_w=a["m_router_w"],
        rb_b2=cat([_np.pad(a["m_router_b"], (0, D - E))[None], a["m_b2"]], axis=0),
        fin=_np.stack([a["a_final_w"], a["a_final_b"]]),
    )
    layout.update(constants())
    nc = _bacc.Bacc("TRN2", target_bir_lowering=False, num_devices=1)
    arrays, args = {}, {}
    for name, v in layout.items():
        v = _np.ascontiguousarray(v)
        arrays[f"in_{name}"] = v
        args[name] = nc.dram_tensor(f"in_{name}", v.shape, _mybir.dt.from_np(v.dtype), kind="ExternalInput").ap()
    args["out"] = nc.dram_tensor("out_0", (B, T, D), _mybir.dt.float32, kind="ExternalOutput").ap()
    build(nc, **args)
    r = _run(nc, [arrays], core_ids=[0])
    return r.results[0]["out_0"]
```
